# Optimizing a Trainium2 kernel written in Bass

```python
import numpy as np
import jax
import jax.numpy as jnp

def _softmax(x, axis=-1):
    return jax.nn.softmax(x, axis=axis)

def _gelu(x):
    return jax.nn.gelu(x, approximate=True)

def _silu(x):
    return jax.nn.silu(x)

def _sigmoid(x):
    return jax.nn.sigmoid(x)

def _layernorm(x, axis=-1, eps=1e-05):
    m = jnp.mean(x, axis=axis, keepdims=True)
    v = jnp.var(x, axis=axis, keepdims=True)
    return (x - m) / jnp.sqrt(v + eps)

def _scatter_add(tgt, idx, src, axis=0):
    return tgt.at[idx].add(src)

def _segment_sum(src, seg, n):
    return jax.ops.segment_sum(src, seg, n)
kernel_name = 'mk_macaron_d1_jaxref_r8_cf4d0b'

def setup_inputs(seed: int=0):
    np.random.seed(seed)
    _w = jnp.asarray

    def _L0_attn_setup():
        import jax, jax.numpy as jnp
        import numpy as np
        B, L, D_MODEL = (2, 256, 128)
        NH, FD = (16, 16)
        HD = D_MODEL // NH
        EPS = 1e-12

        def taylor_exp(x):
            d = x.shape[-1]
            rd = np.sqrt(float(d))
            rrd = np.sqrt(rd)
            r2 = np.sqrt(2.0)
            x2 = (x[..., :, None] * x[..., None, :]).reshape(x.shape[:-1] + (d * d,)) / (rd * r2)
            ones = jnp.ones(x.shape[:-1] + (1,), dtype=x.dtype)
            return jnp.concatenate([ones, x / rrd, x2], axis=-1)
        key = jax.random.key(seed)
        ks = jax.random.split(key, 5)
        x = jax.random.normal(ks[0], (B, L, D_MODEL), dtype=jnp.float32)
        s = 0.02
        Wq = jax.random.normal(ks[1], (D_MODEL, NH * FD), dtype=jnp.float32) * s
        Wk = jax.random.normal(ks[2], (D_MODEL, NH * FD), dtype=jnp.float32) * s
        Wv = jax.random.normal(ks[3], (D_MODEL, NH * HD), dtype=jnp.float32) * s
        Wo = jax.random.normal(ks[4], (NH * HD, D_MODEL), dtype=jnp.float32) * s
        return {'x': x, 'Wq': Wq, 'Wk': Wk, 'Wv': Wv, 'Wo': Wo}
    _L0_attn_in = _L0_attn_setup()

    def _L0_ffn_setup():
        import jax, jax.numpy as jnp
        import numpy as np
        B, S, D, H = (8, 128, 128, 512)
        E, R = (3, 8)
        SCALING = 1.0 / R

        def _mole(x, W, b, A, Bm, Rw):
            gates = jax.nn.softmax(jnp.einsum('bsd,de->bse', x, Rw), axis=-1)
            base = jnp.einsum('bsd,dh->bsh', x, W) + b
            z = jnp.einsum('bsd,edr->ebsr', x, A)
            zg = z * jnp.transpose(gates, (2, 0, 1))[..., None]
            lora = jnp.einsum('ebsr,erh->bsh', zg, Bm)
            return base + SCALING * lora
        key = jax.random.key(seed)
        ks = jax.random.split(key, 12)
        s = lambda k, shape, scale: jax.random.normal(k, shape, dtype=jnp.float32) * scale
        return {'x': s(ks[0], (B, S, D), 1.0), 'W1': s(ks[1], (D, H), D ** (-0.5)), 'b1': jnp.zeros((H,), jnp.float32), 'A1': s(ks[2], (E, D, R), D ** (-0.5)), 'B1': s(ks[3], (E, R, H), 0.0) + s(ks[4], (E, R, H), R ** (-0.5)), 'R1': s(ks[5], (D, E), D ** (-0.5)), 'W2': s(ks[6], (H, D), H ** (-0.5)), 'b2': jnp.zeros((D,), jnp.float32), 'A2': s(ks[7], (E, H, R), H ** (-0.5)), 'B2': s(ks[8], (E, R, D), R ** (-0.5)), 'R2': s(ks[9], (H, E), H ** (-0.5))}
    _L0_ffn_in = _L0_ffn_setup()
    _d = {'L0_attn_x': _L0_attn_in['x'], 'L0_attn_Wq': _L0_attn_in['Wq'], 'L0_attn_Wk': _L0_attn_in['Wk'], 'L0_attn_Wv': _L0_attn_in['Wv'], 'L0_attn_Wo': _L0_attn_in['Wo'], 'L0_ffn_W1': _L0_ffn_in['W1'], 'L0_ffn_b1': _L0_ffn_in['b1'], 'L0_ffn_A1': _L0_ffn_in['A1'], 'L0_ffn_B1': _L0_ffn_in['B1'], 'L0_ffn_R1': _L0_ffn_in['R1'], 'L0_ffn_W2': _L0_ffn_in['W2'], 'L0_ffn_b2': _L0_ffn_in['b2'], 'L0_ffn_A2': _L0_ffn_in['A2'], 'L0_ffn_B2': _L0_ffn_in['B2'], 'L0_ffn_R2': _L0_ffn_in['R2']}
    _x0 = _d['L0_attn_x']
    _d['L0_attn_x'] = jax.random.normal(jax.random.fold_in(jax.random.key(seed), 1), (32, 256, 128), dtype=_x0.dtype)
    del _x0
    return _d

def reference(L0_attn_x, L0_attn_Wq, L0_attn_Wk, L0_attn_Wv, L0_attn_Wo, L0_ffn_W1, L0_ffn_b1, L0_ffn_A1, L0_ffn_B1, L0_ffn_R1, L0_ffn_W2, L0_ffn_b2, L0_ffn_A2, L0_ffn_B2, L0_ffn_R2):

    def _L0_attn_ref(x, Wq, Wk, Wv, Wo):
        import jax, jax.numpy as jnp
        import numpy as np
        B, L, D_MODEL = (2, 256, 128)
        NH, FD = (16, 16)
        HD = D_MODEL // NH
        EPS = 1e-12

        def taylor_exp(x):
            d = x.shape[-1]
            rd = np.sqrt(float(d))
            rrd = np.sqrt(rd)
            r2 = np.sqrt(2.0)
            x2 = (x[..., :, None] * x[..., None, :]).reshape(x.shape[:-1] + (d * d,)) / (rd * r2)
            ones = jnp.ones(x.shape[:-1] + (1,), dtype=x.dtype)
            return jnp.concatenate([ones, x / rrd, x2], axis=-1)
        b, l, _ = x.shape
        q = (x @ Wq).reshape(b, l, NH, FD).transpose(0, 2, 1, 3)
        k = (x @ Wk).reshape(b, l, NH, FD).transpose(0, 2, 1, 3)
        v = (x @ Wv).reshape(b, l, NH, HD).transpose(0, 2, 1, 3)
        qf = taylor_exp(q)
        kf = taylor_exp(k)
        A = jnp.einsum('bhnd,bhmd->bhnm', qf, kf)
        A = jnp.tril(A)
        y = jnp.einsum('bhnm,bhme->bhne', A, v)
        z = 1.0 / (jnp.einsum('bhld,bhld->bhl', qf, jnp.cumsum(kf, axis=2)) + EPS)
        y = y * z[..., None]
        y = y.transpose(0, 2, 1, 3).reshape(b, l, NH * HD)
        return y @ Wo

    def _L0_ffn_ref(x, W1, b1, A1, B1, R1, W2, b2, A2, B2, R2):
        import jax, jax.numpy as jnp
        import numpy as np
        B, S, D, H = (8, 128, 128, 512)
        E, R = (3, 8)
        SCALING = 1.0 / R

        def _mole(x, W, b, A, Bm, Rw):
            gates = jax.nn.softmax(jnp.einsum('bsd,de->bse', x, Rw), axis=-1)
            base = jnp.einsum('bsd,dh->bsh', x, W) + b
            z = jnp.einsum('bsd,edr->ebsr', x, A)
            zg = z * jnp.transpose(gates, (2, 0, 1))[..., None]
            lora = jnp.einsum('ebsr,erh->bsh', zg, Bm)
            return base + SCALING * lora
        h = _mole(x, W1, b1, A1, B1, R1)
        h = jax.nn.relu(h)
        return _mole(h, W2, b2, A2, B2, R2)
    x = L0_attn_x
    x = x + 0.5 * _L0_ffn_ref(_layernorm(x, axis=-1), L0_ffn_W1, L0_ffn_b1, L0_ffn_A1, L0_ffn_B1, L0_ffn_R1, L0_ffn_W2, L0_ffn_b2, L0_ffn_A2, L0_ffn_B2, L0_ffn_R2)
    x = x + _L0_attn_ref(_layernorm(x, axis=-1), L0_attn_Wq, L0_attn_Wk, L0_attn_Wv, L0_attn_Wo)
    x = x + 0.5 * _L0_ffn_ref(_layernorm(x, axis=-1), L0_ffn_W1, L0_ffn_b1, L0_ffn_A1, L0_ffn_B1, L0_ffn_R1, L0_ffn_W2, L0_ffn_b2, L0_ffn_A2, L0_ffn_B2, L0_ffn_R2)
    return x

_drawn_inputs = setup_inputs


def setup_inputs(seed=0):
    import zlib

    import numpy as np

    out = dict(_drawn_inputs(seed))
    spreads = {'L0_ffn_b1': (0.0, 0.1), 'L0_ffn_b2': (0.0, 0.1)}
    factors = {'L0_attn_Wq': 8.0,
     'L0_attn_Wk': 8.0,
     'L0_attn_Wv': 4.787,
     'L0_attn_Wo': 5.316,
     'L0_ffn_R2': 3.334}
    for name, (base, spread) in spreads.items():
        noise = np.random.default_rng([zlib.crc32(name.encode()), seed]).standard_normal(out[name].shape)
        drawn = base * np.exp(spread * noise) if base else spread * noise
        out[name] = jnp.asarray(drawn.astype(out[name].dtype))
    for name, factor in factors.items():
        out[name] = (out[name] * factor).astype(out[name].dtype)
    return out
```

```python
from contextlib import ExitStack

import concourse.bass as bass
from concourse import mybir

F32 = mybir.dt.float32
F16 = mybir.dt.float16
ALU = mybir.AluOpType
ACT = mybir.ActivationFunctionType
AX = mybir.AxisListType

P = 128
BATCH, LEN, D = 32, 256, 128
TILES = BATCH * LEN // P
GT = 4
GN = GT * P
GROUPS = TILES // GT
HID = 512
HC = HID // P
E, R = 3, 8
ER = E * R
YW = D + ER + E
ZW = ER + E
SB = 32
SK = 3 * SB
LN_EPS = 1e-5
WS = 4.0
GATE_LINKS = 6
ST = LEN // P
NH, FD, HD = 16, 16, 8
SW = LEN + P
ATT_EPS = 1e-12


def split(e, hi, lo, src, scale, sem, base):
    e.tensor_scalar(hi, src, scale, None, ALU.mult).then_inc(sem, 1)
    e.wait_ge(sem, base + 1)
    e.scalar_tensor_tensor(out=lo, in0=src, scalar=scale, in1=hi, op0=ALU.mult, op1=ALU.subtract).then_inc(sem, 1)
    e.wait_ge(sem, base + 2)


def wait_alone(e, semaphore, value, started):
    if not isinstance(value, int):
        value = e.to_reg(value)
    e.wait_ge(started, 1)
    e.wait_ge(semaphore, value)


class FeedForward:

    def __init__(self, nc, ctx, name, mem):
        sem = lambda what: ctx.enter_context(nc.semaphore(f"{name}_{what}"))
        self.m = mem
        self.mean_var = sem("mean_var")
        self.rstd = sem("rstd")
        self.xn = sem("xn")
        self.xT_ps = sem("xT_ps")
        self.xT_hi = sem("xT_hi")
        self.xT_lo = sem("xT_lo")
        self.z_ps = [sem("z1_ps"), sem("z2_ps")]
        self.logits = [sem("logits1"), sem("logits2")]
        self.exps = [sem("exps1"), sem("exps2")]
        self.zs = [sem("zs1"), sem("zs2")]
        self.zsT_ps = [sem("zsT1_ps"), sem("zsT2_ps")]
        self.zsT = [sem("zsT1"), sem("zsT2")]
        self.h_ps = sem("h_ps")
        self.h_hi = sem("h_hi")
        self.h_lo = sem("h_lo")
        self.y_ps = sem("y_ps")
        self.done = sem("done")
        self.stats = sem("stats")
        self.gate_chain = [sem("gate_chain1"), sem("gate_chain2")]
        self.pool_chain = sem("pool_chain")

    def dve_stats(self, e, g, p, x_ready):
        m = self.m
        x_ready(e, g)
        for t in range(GT):
            last = e.bn_stats(m.bn[:, p, t, :], m.x[:, bass.ds(g * GN + t * P, P)])
        last.then_inc(self.stats, 1)
        wait_alone(e, self.stats, g + 1, m.started)
        for t in range(GT):
            last = e.bn_aggr(m.mv[:, p, t, :], m.bn[:, p, t, :])
        last.then_inc(self.mean_var, 1)

    def dve_norm(self, e, g, p, skip):
        m = self.m
        e.wait_ge(self.rstd, g + 1)
        if not skip:
            e.wait_ge(self.xT_ps, g)
        for t in range(GT):
            last = e.tensor_scalar(m.xn[:, t, :], m.x[:, bass.ds(g * GN + t * P, P)],
                                   m.mv[:, p, t, 0:1], m.rs[:, p, t:t + 1], ALU.subtract, ALU.mult)
        last.then_inc(self.xn, 1)

    def dve_xT_lo(self, e, g, p):
        m = self.m
        e.wait_ge(self.xT_hi, g + 1)
        e.tensor_tensor(m.xl[:, p, :], m.psT[:, :], m.xh[:, p, :], ALU.subtract).then_inc(self.xT_lo, 1)

    def dve_gates(self, e, g, layer):
        m = self.m
        chain, n = self.gate_chain[layer], [0]

        def link(ins):
            n[0] += 1
            ins.then_inc(chain, 1)
            e.wait_ge(chain, g * GATE_LINKS + n[0])

        e.wait_ge(self.z_ps[layer], g + 1)
        z, lg = m.z_views[layer]
        mx, sm, ex, gt, zg, zs = m.mx[layer], m.sm[layer], m.ex[layer], m.gt[layer], m.zg[layer], m.zs[layer]
        for half, (a, b) in enumerate(m.halves[layer]):
            last = e.tensor_reduce(mx[:, a:b], lg[half], AX.X, ALU.max)
        link(last)
        for half, (a, b) in enumerate(m.halves[layer]):
            last = e.tensor_tensor(m.lg[layer][:, a:b, :], lg[half],
                                   mx[:, a:b].unsqueeze(2).broadcast_to([P, b - a, E]), ALU.subtract)
        last.then_inc(self.logits[layer], 1)
        e.wait_ge(self.exps[layer], g + 1)
        link(e.tensor_reduce(sm[:, :], ex[:, :, :], AX.X, ALU.add))
        link(e.reciprocal(sm[:, :], sm[:, :]))
        link(e.tensor_tensor(gt[:, :, :], ex[:, :, :], sm[:, :].unsqueeze(2).broadcast_to([P, GT, E]), ALU.mult))
        for half, (a, b) in enumerate(m.halves[layer]):
            last = e.tensor_tensor(zg[:, a:b, :].rearrange("p t (e r) -> p t e r", r=R), z[half],
                                   gt[:, a:b, :].unsqueeze(3).broadcast_to([P, b - a, E, R]), ALU.mult)
        link(last)
        link(e.tensor_copy(zs[:, :, 0:3:2, 0:ER], zg[:, :, :].unsqueeze(2).broadcast_to([P, GT, 2, ER])))
        e.tensor_tensor(zs[:, :, 1, 0:ER], zg[:, :, :], zs[:, :, 0, 0:ER], ALU.subtract).then_inc(self.zs[layer], 1)

    def dve_h_lo(self, e, g, pair):
        m = self.m
        e.wait_ge(self.h_hi, 2 * g + pair + 1)
        e.scalar_tensor_tensor(out=m.hl[:, 2 * pair:2 * pair + 2, :], in0=m.psH[pair][:, :, :], scalar=0.0,
                               in1=m.hh[:, 2 * pair:2 * pair + 2, :], op0=ALU.max,
                               op1=ALU.subtract).then_inc(self.h_lo, 1)

    def dve_residual(self, e, g):
        m = self.m
        e.wait_ge(self.y_ps, g + 1)
        for half in range(2):
            xg = m.x[:, bass.ds(g * GN + half * 2 * P, 2 * P)].rearrange("p (t d) -> p t d", d=D)
            last = e.scalar_tensor_tensor(out=xg, in0=m.psY[:, half, :, 0:D], scalar=0.5 / (WS * WS), in1=xg,
                                          op0=ALU.mult, op1=ALU.add)
        last.then_inc(self.done, 1)

    def vector(self, e, x_ready):
        def step(g, p, prev, main, nxt, first=False):
            if nxt:
                self.dve_stats(e, g + 1, 1 - p, x_ready)
            if prev:
                self.dve_gates(e, g - 1, 1)
            if nxt:
                self.dve_norm(e, g + 1, 1 - p, skip=first)
            if main:
                self.dve_h_lo(e, g, 0)
            if prev:
                self.dve_residual(e, g - 1)
            if nxt:
                self.dve_xT_lo(e, g + 1, 1 - p)
            if main:
                self.dve_h_lo(e, g, 1)
            if nxt:
                self.dve_gates(e, g + 1, 0)
        run_steps(e, step, GROUPS)

    def scalar(self, e):
        m = self.m

        def xT_hi(g, p):
            e.wait_ge(self.xT_ps, g + 1)
            e.activation(m.xh[:, p, :], m.psT[:, :], ACT.Copy).then_inc(self.xT_hi, 1)

        def exps(g, layer):
            e.wait_ge(self.logits[layer], g + 1)
            e.activation(m.ex[layer][:, :, :], m.lg[layer][:, :, :], ACT.Exp,
                         scale=WS ** -(layer + 1)).then_inc(self.exps[layer], 1)

        def zsT(g, layer):
            e.wait_ge(self.zsT_ps[layer], g + 1)
            e.activation(m.zsT[layer][:, :], m.psZT[0:SK, :], ACT.Copy).then_inc(self.zsT[layer], 1)

        def h_hi(g, pair):
            e.wait_ge(self.h_ps, 2 * g + pair + 1)
            e.activation(m.hh[:, 2 * pair:2 * pair + 2, :], m.psH[pair][:, :, :], ACT.Relu).then_inc(self.h_hi, 1)

        def step(g, p, prev, main, nxt, first=False):
            if prev:
                exps(g - 1, 1)
            if main:
                h_hi(g, 0)
            if prev:
                zsT(g - 1, 1)
            if nxt:
                xT_hi(g + 1, 1 - p)
            if main:
                h_hi(g, 1)
            if nxt:
                exps(g + 1, 0)
                zsT(g + 1, 0)
        run_steps(e, step, GROUPS)

    def gpsimd(self, e):
        m = self.m

        def step(g, p, prev, main, nxt, first=False):
            if nxt:
                wait_alone(e, self.mean_var, g + 2, m.started)
                e.tensor_scalar(m.ve[:, 0:GT], m.mv[:, 1 - p, :, 1], LN_EPS, None, ALU.add).then_inc(self.pool_chain, 1)
                e.wait_ge(self.pool_chain, g + 2)
                e.tensor_tensor(m.rs[:, 1 - p, :], m.ve[:, 0:GT], m.neg_half[:, 0:GT], ALU.pow).then_inc(self.rstd, 1)
        run_steps(e, step, GROUPS)

    def tensor(self, e):
        m = self.m

        def mm(out, lhsT, rhs, start, stop):
            return e.matmul(out, lhsT, rhs, start=start, stop=stop, skip_group_check=True)

        def xT(g, p, first):
            e.wait_ge(self.xn, g + 1)
            if not first:
                e.wait_ge(self.xT_lo, g)
            for t in range(GT):
                last = e.transpose(m.psT[:, t * P:(t + 1) * P], m.xn[:, t, :], m.ident32[:, :])
            last.then_inc(self.xT_ps, 1)

        def z1(g, p, tail):
            if tail:
                e.wait_ge(self.zsT[1], g - 1)
            for t in range(GT):
                out, tok = m.psZ[:, t, :], slice(t * P, (t + 1) * P)
                e.wait_ge(self.xT_hi, g + 1)
                mm(out, m.xh[:, p, tok], m.arh[:, :], t == 0, False)
                mm(out, m.xh[:, p, tok], m.arl[:, :], False, False)
                e.wait_ge(self.xT_lo, g + 1)
                last = mm(out, m.xl[:, p, tok], m.arh[:, :], False, True)
            last.then_inc(self.z_ps[0], 1)

        def zsT(g, layer, other):
            e.wait_ge(self.zs[layer], g + 1)
            if other is not None:
                e.wait_ge(self.zsT[1 - layer], other)
            for t in range(GT):
                last = e.transpose(m.psZT[0:SK, t * P:(t + 1) * P],
                                   m.zs[layer][:, t, :, :].rearrange("p k c -> p (k c)"), m.ident16[:, :])
            last.then_inc(self.zsT_ps[layer], 1)

        def hidden(g, p, pair, first):
            if not first:
                e.wait_ge(self.h_lo, 2 * (g - 1) + pair + 1)
            e.wait_ge(self.xT_lo, g + 1)
            for i in range(2):
                c, out = slice((2 * pair + i) * P, (2 * pair + i + 1) * P), m.psH[pair][:, i, :]
                mm(out, m.w1h[:, c], m.xh[:, p, :], True, False)
                mm(out, m.w1l[:, c], m.xh[:, p, :], False, False)
                mm(out, m.w1h[:, c], m.xl[:, p, :], False, False)
            e.wait_ge(self.zsT[0], g + 1)
            for i in range(2):
                c, out = slice((2 * pair + i) * P, (2 * pair + i + 1) * P), m.psH[pair][:, i, :]
                last = mm(out, m.b1s[:, c], m.zsT[0][:, :], False, True)
            last.then_inc(self.h_ps, 1)

        def second(g, pair, first):
            if pair == 0 and not first:
                e.wait_ge(self.done, g)
            for c in (2 * pair, 2 * pair + 1):
                for t in range(GT):
                    out, tok = m.psY[:, t // 2, t % 2, 0:YW], slice(t * P, (t + 1) * P)
                    if t == 0:
                        e.wait_ge(self.h_lo, 2 * g + pair + 1)
                    mm(out, m.hh[:, c, tok], m.w2h[:, c, :], c == 0 and t % 2 == 0, False)
                    mm(out, m.hh[:, c, tok], m.w2l[:, c, :], False, False)
                    last = mm(out, m.hl[:, c, tok], m.w2h[:, c, :], False, c == HC - 1)
            if pair == 1:
                last.then_inc(self.z_ps[1], 1)

        def adapters2(g):
            e.wait_ge(self.zsT[1], g + 1)
            for t in range(GT):
                last = mm(m.psY[:, t // 2, t % 2, 0:D], m.zsT[1][:, t * P:(t + 1) * P], m.b2s[:, :], False, True)
            last.then_inc(self.y_ps, 1)

        def step(g, p, prev, main, nxt, first=False):
            if main:
                hidden(g, p, 0, first=isinstance(g, int) and g == 0)
            if prev:
                zsT(g - 1, 1, g + 1 if main else None)
            if nxt:
                xT(g + 1, 1 - p, first)
            if prev:
                adapters2(g - 1)
            if main:
                hidden(g, p, 1, first=isinstance(g, int) and g == 0)
                second(g, 0, first=isinstance(g, int) and g == 0)
            if nxt:
                z1(g + 1, 1 - p, tail=prev)
            if main:
                second(g, 1, first=False)
            if nxt:
                zsT(g + 1, 0, g if prev else None)
        run_steps(e, step, GROUPS)


class Attention:

    def __init__(self, nc, ctx, name, mem):
        sem = lambda what: ctx.enter_context(nc.semaphore(f"{name}_{what}"))
        self.m = mem
        self.stats = sem("stats")
        self.mean_var = sem("mean_var")
        self.pool_chain = sem("pool_chain")
        self.rstd = sem("rstd")
        self.xn = sem("xn")
        self.xT_ps = sem("xT_ps")
        self.xT_hi = sem("xT_hi")
        self.xT_lo = sem("xT_lo")
        self.q_ps = sem("q_ps")
        self.q_hi = sem("q_hi")
        self.q_st = sem("q_st")
        self.k_ps = sem("k_ps")
        self.k_hi = sem("k_hi")
        self.k_lo = sem("k_lo")
        self.v_ps = sem("v_ps")
        self.v_hi = sem("v_hi")
        self.v_lo = sem("v_lo")
        self.s_ps = sem("s_ps")
        self.squares = sem("squares")
        self.masked = sem("masked")
        self.sums_ps = sem("sums_ps")
        self.sums = sem("sums")
        self.ytok_ps = sem("ytok_ps")
        self.y_chain = sem("y_chain")
        self.y = sem("y")
        self.yT_ps = sem("yT_ps")
        self.yT_hi = sem("yT_hi")
        self.yT_lo = sem("yT_lo")
        self.out_ps = sem("out_ps")
        self.done = sem("done")

    def vector(self, e):
        m = self.m

        def tile(b, t):
            return m.x[:, bass.ds(b * LEN + t * P, P)]

        def stats(b):
            for t in range(ST):
                last = e.bn_stats(m.bn[:, 0, t, :], tile(b, t))
            last.then_inc(self.stats, 1)
            wait_alone(e, self.stats, b + 1, m.started)
            for t in range(ST):
                last = e.bn_aggr(m.mv[:, 0, t, :], m.bn[:, 0, t, :])
            last.then_inc(self.mean_var, 1)

        def norm(b, skip):
            e.wait_ge(self.rstd, b + 1)
            if not skip:
                e.wait_ge(self.xT_ps, b)
            for t in range(ST):
                last = e.tensor_scalar(m.xn[:, t, :], tile(b, t), m.mv[:, 0, t, 0:1], m.rs[:, 0, t:t + 1],
                                       ALU.subtract, ALU.mult)
            last.then_inc(self.xn, 1)

        def xT_lo(b):
            e.wait_ge(self.xT_hi, b + 1)
            e.tensor_tensor(m.axl[:, :], m.psT[:, 0:LEN], m.axh[:, :], ALU.subtract).then_inc(self.xT_lo, 1)

        def q_stack(b, p):
            e.wait_ge(self.q_hi, b + 1)
            e.scalar_tensor_tensor(out=m.qs[:, p, :, :], in0=m.psJ, scalar=m.lo_rows[:, 0:1], in1=m.qh[:, :, :],
                                   op0=ALU.mult, op1=ALU.add).then_inc(self.q_st, 1)

        def k_lo(b, p):
            e.wait_ge(self.k_hi, b + 1)
            e.tensor_tensor(m.kl[:, p, :, :], m.psJ, m.kh[:, p, :, :], ALU.subtract).then_inc(self.k_lo, 1)

        def v_lo(b, p):
            e.wait_ge(self.v_hi, b + 1)
            e.tensor_tensor(m.vl[:, p, :, :, 0:HD], m.psV, m.vh[:, p, :, :, 0:HD], ALU.subtract).then_inc(self.v_lo, 1)

        def normalise(b):
            n = b * 2
            e.wait_ge(self.ytok_ps, b + 1)
            e.tensor_scalar(m.den[:, :, :], m.psYt[:, :, :, HD], 2 * WS * ATT_EPS, None, ALU.add).then_inc(self.y_chain, 1)
            e.wait_ge(self.y_chain, n + 1)
            e.reciprocal(m.den[:, :, :], m.den[:, :, :]).then_inc(self.y_chain, 1)
            e.wait_ge(self.y_chain, n + 2)
            e.tensor_tensor(m.yn[:, :, :, :], m.psYt[:, :, :, 0:HD],
                            m.den[:, :, :].unsqueeze(3).broadcast_to([P, ST, NH, HD]), ALU.mult).then_inc(self.y, 1)

        def yT_lo(b):
            e.wait_ge(self.yT_hi, b + 1)
            e.tensor_tensor(m.yl[:, :], m.psT[:, 0:LEN], m.yh[:, :], ALU.subtract).then_inc(self.yT_lo, 1)

        def residual(b):
            e.wait_ge(self.out_ps, b + 1)
            xb = m.x[:, bass.ds(b * LEN, LEN)]
            e.scalar_tensor_tensor(out=xb, in0=m.psT[:, LEN:2 * LEN], scalar=1.0 / WS, in1=xb, op0=ALU.mult,
                                   op1=ALU.add).then_inc(self.done, 1)

        def step(b, p, prev, main, nxt, first=False):
            if nxt:
                stats(b + 1)
                norm(b + 1, first)
                xT_lo(b + 1)
            if prev:
                normalise(b - 1)
            if nxt:
                v_lo(b + 1, 1 - p)
                q_stack(b + 1, 1 - p)
            if prev:
                yT_lo(b - 1)
            if nxt:
                k_lo(b + 1, 1 - p)
            if prev:
                residual(b - 1)
        run_steps(e, step, BATCH)

    def scalar(self, e):
        m = self.m

        def square(b, k, first):
            e.wait_ge(self.s_ps, 8 * b + k + 1)
            if not first:
                e.wait_ge(self.sums_ps, 4 * (b - 1) + k // 2 + 1)
            e.activation(m.G[:, k, :, :], m.psS[k % 2][:, :, 0:SW], ACT.Square, bias=1.0,
                         scale=0.25 / (WS * WS)).then_inc(self.squares, 1)

        def sums(b, half):
            e.wait_ge(self.sums_ps, 4 * b + 2 * half + 2)
            e.activation(m.YT[:, 2 * half:2 * half + 2, :], m.psU, ACT.Copy).then_inc(self.sums, 1)

        def xT_hi(b):
            e.wait_ge(self.xT_ps, b + 1)
            e.activation(m.axh[:, :], m.psT[:, 0:LEN], ACT.Copy).then_inc(self.xT_hi, 1)

        def v_hi(b, p):
            e.wait_ge(self.v_ps, b + 1)
            e.activation(m.vf[:, p, :, :, 0:HD], m.psV, ACT.Copy)
            e.activation(m.vh[:, p, :, :, 0:HD], m.psV, ACT.Copy).then_inc(self.v_hi, 1)

        def q_hi(b):
            e.wait_ge(self.q_ps, b + 1)
            e.activation(m.qh[:, :, :], m.psJ, ACT.Copy).then_inc(self.q_hi, 1)

        def k_hi(b, p):
            e.wait_ge(self.k_ps, b + 1)
            e.activation(m.kh[:, p, :, :], m.psJ, ACT.Copy).then_inc(self.k_hi, 1)

        def yT_hi(b):
            e.wait_ge(self.yT_ps, b + 1)
            e.activation(m.yh[:, :], m.psT[:, 0:LEN], ACT.Copy).then_inc(self.yT_hi, 1)

        def step(b, p, prev, main, nxt, first=False):
            zero = isinstance(b, int) and b == 0
            if main:
                square(b, 0, zero)
                square(b, 1, zero)
            if prev:
                sums(b - 1, 1)
            if nxt:
                xT_hi(b + 1)
            if main:
                square(b, 2, zero)
                square(b, 3, zero)
                square(b, 4, zero)
            if nxt:
                v_hi(b + 1, 1 - p)
            if main:
                square(b, 5, zero)
            if nxt:
                q_hi(b + 1)
            if main:
                square(b, 6, zero)
                sums(b, 0)
            if prev:
                yT_hi(b - 1)
            if main:
                square(b, 7, zero)
            if nxt:
                k_hi(b + 1, 1 - p)
        run_steps(e, step, BATCH)

    def gpsimd(self, e):
        m = self.m

        def step(b, p, prev, main, nxt, first=False):
            if nxt:
                wait_alone(e, self.mean_var, b + 2, m.started)
                e.tensor_scalar(m.ve[:, 0:ST], m.mv[:, 0, 0:ST, 1], LN_EPS, None, ALU.add).then_inc(self.pool_chain, 1)
                e.wait_ge(self.pool_chain, b + 2)
                e.tensor_tensor(m.rs[:, 0, 0:ST], m.ve[:, 0:ST], m.neg_half[:, 0:ST], ALU.pow).then_inc(self.rstd, 1)
            if main:
                for k in range(NH // 2):
                    wait_alone(e, self.squares, 8 * b + k + 1, m.started)
                    for h in range(2):
                        g = m.G[:, k, h, :].rearrange("p (c n) -> p c n", n=P)[:, 0:3:2, :]
                        last = e.affine_select(out=g, in_=g, compare_op=ALU.is_ge, fill=0.0, base=0,
                                               pattern=[[0, 2], [1, P]], channel_multiplier=-1)
                    last.then_inc(self.masked, 1)
        run_steps(e, step, BATCH)

    def tensor(self, e):
        m = self.m

        def mm(out, lhsT, rhs, start, stop, **kw):
            return e.matmul(out, lhsT, rhs, start=start, stop=stop, skip_group_check=True, **kw)

        def xT(b, free):
            e.wait_ge(self.xn, b + 1)
            if free:
                e.wait_ge(self.done, b - 2)
            for t in range(ST):
                last = e.transpose(m.psT[:, t * P:(t + 1) * P], m.xn[:, t, :], m.ident32[:, :])
            last.then_inc(self.xT_ps, 1)

        def v(b):
            e.wait_ge(self.xT_lo, b + 1)
            for t in range(ST):
                out, tok = m.psT[:, LEN + t * P:LEN + (t + 1) * P], slice(t * P, (t + 1) * P)
                mm(out, m.axh[:, tok], m.wvh[:, :], t == 0, False)
                mm(out, m.axh[:, tok], m.wvl[:, :], False, False)
                last = mm(out, m.axl[:, tok], m.wvh[:, :], False, True)
            last.then_inc(self.v_ps, 1)

        def project(wh, wl, done):
            for j in range(4):
                out, c = m.psJ[:, j, :], slice(j * P, (j + 1) * P)
                mm(out, wh[:, c], m.axh[:, :], j % 2 == 0, False)
                mm(out, wl[:, c], m.axh[:, :], False, False)
                last = mm(out, wh[:, c], m.axl[:, :], False, True)
            last.then_inc(done, 1)

        def scores(b, p, k, first):
            if k < 2:
                if not first:
                    e.wait_ge(self.squares, 8 * b + k - 1)
            else:
                e.wait_ge(self.squares, 8 * b + k - 1)
            if k == 0:
                e.wait_ge(self.q_st, b + 1)
                e.wait_ge(self.k_lo, b + 1)
            for h in range(2):
                j, i = k // 2, 2 * (k % 2) + h
                rows = slice(32 * i, 32 * i + 32)
                for kt, (n0, n1, c0) in enumerate(((0, LEN, 0), (P, LEN, LEN))):
                    for w, kk in enumerate((m.kh, m.kl)):
                        last = mm(m.psS[k % 2][:, h, c0:c0 + n1 - n0], kk[rows, p, j, kt * P:(kt + 1) * P],
                                  m.qs[rows, p, j, n0:n1], kt == 0 and w == 0, kt == 1 and w == 1,
                                  tile_position=(32 * i, 0))
            last.then_inc(self.s_ps, 1)

        def head_sums(b, p, j, free):
            e.wait_ge(self.masked, 8 * b + 2 * j + 2)
            if j == 0:
                e.wait_ge(self.v_lo, b + 1)
                if free:
                    e.wait_ge(self.sums, 2 * b)
            if j == 2:
                e.wait_ge(self.sums, 2 * b + 1)
            out = m.psU[:, j % 2, :]
            heads = slice(4 * j, 4 * j + 4)
            for kt, n0 in ((0, 0), (1, P)):
                for w, vv in enumerate((m.vh, m.vl)):
                    mm(out[:, n0:LEN], vv[:, p, kt, heads, :].rearrange("p h c -> p (h c)"), m.ones_tri[:, 0:LEN - n0],
                       kt == 0 and w == 0, False)
            for kt, n0, c0 in ((0, 0, 0), (1, P, LEN)):
                for i in range(4):
                    last = mm(out[32 * i:32 * i + 32, n0:LEN], m.vf[:, p, kt, 4 * j + i, :],
                              m.G[:, 2 * j + i // 2, i % 2, c0:c0 + LEN - n0], False, kt == 1,
                              tile_position=(0, 32 * i))
            last.then_inc(self.sums_ps, 1)

        def ytok(b, free):
            e.wait_ge(self.sums, 2 * b + 2)
            if free:
                e.wait_ge(self.k_lo, b + 2)
            for t in range(ST):
                for j in range(4):
                    last = e.transpose(m.psYf[:, t, j, :], m.YT[:, j, t * P:(t + 1) * P], m.ident32[:, :])
            last.then_inc(self.ytok_ps, 1)

        def yT(b):
            e.wait_ge(self.y, b + 1)
            for t in range(ST):
                last = e.transpose(m.psT[:, t * P:(t + 1) * P], m.yn[:, t, :, :].rearrange("p h c -> p (h c)"),
                                   m.ident32[:, :])
            last.then_inc(self.yT_ps, 1)

        def output(b):
            e.wait_ge(self.yT_lo, b + 1)
            for t in range(ST):
                out, tok = m.psT[:, LEN + t * P:LEN + (t + 1) * P], slice(t * P, (t + 1) * P)
                mm(out, m.yh[:, tok], m.woh[:, :], t == 0, False)
                mm(out, m.yh[:, tok], m.wol[:, :], False, False)
                last = mm(out, m.yl[:, tok], m.woh[:, :], False, True)
            last.then_inc(self.out_ps, 1)

        def step(b, p, prev, main, nxt, first=False):
            zero = isinstance(b, int) and b == 0
            if main:
                scores(b, p, 0, zero)
                scores(b, p, 1, zero)
            if prev:
                head_sums(b - 1, 1 - p, 3, True)
            if nxt:
                xT(b + 1, not (isinstance(b, int) and b < 2))
            if main:
                scores(b, p, 2, zero)
            if prev:
                ytok(b - 1, main)
            if main:
                scores(b, p, 3, zero)
                head_sums(b, p, 0, not zero)
            if nxt:
                v(b + 1)
            if main:
                scores(b, p, 4, zero)
            if nxt:
                if prev:
                    e.wait_ge(self.y, b)
                elif main:
                    e.wait_ge(self.k_lo, b + 1)
                project(m.wqh, m.wql, self.q_ps)
            if main:
                scores(b, p, 5, zero)
                head_sums(b, p, 1, not zero)
            if prev:
                if nxt:
                    e.wait_ge(self.v_lo, b + 2)
                yT(b - 1)
            if main:
                scores(b, p, 6, zero)
            if nxt:
                e.wait_ge(self.q_st, b + 2)
                project(m.wkh, m.wkl, self.k_ps)
            if main:
                scores(b, p, 7, zero)
                head_sums(b, p, 2, not zero)
            if prev:
                output(b - 1)
        run_steps(e, step, BATCH)


def run_steps(e, step, count):
    step(-1, 1, False, False, True, first=True)
    step(0, 0, False, True, True)
    step(1, 1, True, True, True)
    with e.Fori(2, count - 2, 2) as g:
        step(g, 0, True, True, True)
        step(g + 1, 1, True, True, True)
    step(count - 2, 0, True, True, True)
    step(count - 1, 1, True, True, False)
    step(count, 0, True, False, False)


class Memory:
    pass


def program(nc, x, Wq, Wk, Wv, Wo, W1, b1, A1, B1, R1, W2, b2, A2, B2, R2, out):
    with ExitStack() as ctx:
        m = Memory()

        def sb(name, shape, dt):
            return ctx.enter_context(nc.sbuf_tensor(name, shape, dt))

        def ps(name, shape, dt=F32):
            return ctx.enter_context(nc.psum_tensor(name, shape, dt))

        def sem(name):
            return ctx.enter_context(nc.semaphore(name))

        m.x = sb("x_sb", [P, TILES * D], F32)
        w1_in = sb("w1_in", [P, HID], F32)
        ar_in = sb("ar_in", [P, ZW], F32)
        w2_in = sb("w2_in", [P, HC, YW], F32)
        b1_in = sb("b1_in", [SK, HID], F32)
        b2_in = sb("b2_in", [SK, D], F32)
        row_scale = sb("row_scale", [SK, 2], F32)
        b1_sc = sb("b1_sc", [SK, HID], F32)
        b2_sc = sb("b2_sc", [SK, D], F32)
        m.w1h, m.w1l = sb("w1h", [P, HID], F16), sb("w1l", [P, HID], F16)
        m.arh, m.arl = sb("arh", [P, ZW], F16), sb("arl", [P, ZW], F16)
        m.w2h, m.w2l = sb("w2h", [P, HC, YW], F16), sb("w2l", [P, HC, YW], F16)
        m.b1s, m.b2s = sb("b1s", [SK, HID], F16), sb("b2s", [SK, D], F16)
        m.ident32, m.ident16 = sb("ident32", [P, P], F32), sb("ident16", [P, P], F16)
        m.neg_half = sb("neg_half", [P, GT], F32)
        m.bn = sb("bn", [P, 2, GT, 6], F32)
        m.mv = sb("mv", [P, 2, GT, 2], F32)
        m.ve = sb("ve", [P, GT], F32)
        m.rs = sb("rs", [P, 2, GT], F32)
        m.xn = sb("xn", [P, GT, D], F32)
        m.xh, m.xl = sb("xh", [P, 2, GN], F16), sb("xl", [P, 2, GN], F16)
        two = range(2)
        m.mx = [sb(f"mx{i}", [P, GT], F32) for i in two]
        m.lg = [sb(f"lg{i}", [P, GT, E], F32) for i in two]
        m.ex = [sb(f"ex{i}", [P, GT, E], F32) for i in two]
        m.sm = [sb(f"sm{i}", [P, GT], F32) for i in two]
        m.gt = [sb(f"gt{i}", [P, GT, E], F32) for i in two]
        m.zg = [sb(f"zg{i}", [P, GT, ER], F32) for i in two]
        m.zs = [sb(f"zs{i}", [P, GT, 3, SB], F16) for i in two]
        m.zsT = [sb(f"zsT{i}", [SK, GN], F16) for i in two]
        m.hh, m.hl = sb("hh", [P, HC, GN], F16), sb("hl", [P, HC, GN], F16)

        aw_in = sb("aw_in", [P, 2 * NH * FD + 2 * D], F32)
        m.wqh, m.wql = sb("wqh", [P, NH * 2 * FD], F16), sb("wql", [P, NH * 2 * FD], F16)
        m.wkh, m.wkl = sb("wkh", [P, NH * 2 * FD], F16), sb("wkl", [P, NH * 2 * FD], F16)
        m.wvh, m.wvl = sb("wvh", [P, D], F16), sb("wvl", [P, D], F16)
        m.woh, m.wol = sb("woh", [P, D], F16), sb("wol", [P, D], F16)
        steps_in = sb("steps_in", [P, 8], F32)
        m.lo_rows = sb("lo_rows", [P, 1], F32)
        m.ones_tri = sb("ones_tri", [P, LEN], F16)
        m.axh, m.axl = sb("axh", [P, LEN], F16), sb("axl", [P, LEN], F16)
        m.qh, m.qs = sb("qh", [P, 4, LEN], F16), sb("qs", [P, 2, 4, LEN], F16)
        m.kh, m.kl = sb("kh", [P, 2, 4, LEN], F16), sb("kl", [P, 2, 4, LEN], F16)
        m.vf = sb("vf", [P, 2, ST, NH, 32], F32)
        m.vh, m.vl = sb("vh", [P, 2, ST, NH, 32], F16), sb("vl", [P, 2, ST, NH, 32], F16)
        m.G = sb("G", [P, NH // 2, 2, SW], F32)
        m.YT = sb("YT", [P, 4, LEN], F32)
        m.den = sb("den", [P, ST, NH], F32)
        m.yn = sb("yn", [P, ST, NH, HD], F32)
        m.yh, m.yl = sb("yh", [P, LEN], F16), sb("yl", [P, LEN], F16)

        m.psH = [ps(f"psH{i}", [P, 2, GN]) for i in two]
        m.psY = ps("psY", [P, 2, 2, 2 * P])
        m.psT = ps("psT", [P, GN])
        bank = ps("psB", [P, GN])
        m.psZ = bank[:, 0:GT * SB].rearrange("p (t c) -> p t c", c=SB)[:, :, 0:ZW]
        m.psZT = bank[:, GN // 2:GN].bitcast(F16)
        m.psJ = m.psH[0][:, :, :].rearrange("p a (b n) -> p (a b) n", n=LEN)
        m.psYf = m.psH[0][:, :, :].rearrange("p t (j c) -> p t j c", c=P)
        m.psYt = m.psH[0][:, :, :].rearrange("p t (h c) -> p t h c", c=32)
        m.psS = [m.psH[1][:, :, :], m.psY[:, :, :, :].rearrange("p a b n -> p a (b n)")]
        m.psV = m.psT[:, LEN:2 * LEN].rearrange("p (t h c) -> p t h c", h=NH, c=HD)
        m.psU = bank[:, :].rearrange("p (j n) -> p j n", n=LEN)
        m.halves = [[(0, GT)], [(0, 2), (2, 4)]]
        m.z_views = [
            ([m.psZ[:, :, 0:ER].rearrange("p t (e r) -> p t e r", r=R)], [m.psZ[:, :, ER:ZW]]),
            ([m.psY[:, h, :, D:D + ER].rearrange("p t (e r) -> p t e r", r=R) for h in two],
             [m.psY[:, h, :, D + ER:YW] for h in two]),
        ]

        w_in = sem("w_in")
        x_in = [sem(f"x_in{i}") for i in range(4)]
        consts = sem("consts")
        m.started = sem("started")
        prep = sem("prep")
        ready = sem("ready")
        stored = sem("stored")
        ff1 = FeedForward(nc, ctx, "ff1", m)
        att = Attention(nc, ctx, "att", m)
        ff2 = FeedForward(nc, ctx, "ff2", m)

        block = ctx.enter_context(nc.Block())

        @block.sync
        def _(sp):
            xt = x.rearrange("b l d -> (b l) d").rearrange("(t p) d -> p t d", p=P)
            xs = m.x[:, :].rearrange("p (t d) -> p t d", d=D)
            q = TILES // 4
            sp.dma_start(xs[:, 0:q, :], xt[:, 0:q, :]).then_inc(x_in[0], 16)
            sp.dma_start(w1_in[:, :], W1).then_inc(w_in, 16)
            sp.dma_start(ar_in[:, 0:ER].rearrange("p (e r) -> p e r", r=R), A1.rearrange("e d r -> d e r")).then_inc(w_in, 16)
            sp.dma_start(ar_in[:, ER:ZW], R1).then_inc(w_in, 16)
            for c in range(HC):
                rows = slice(c * P, (c + 1) * P)
                sp.dma_start(w2_in[:, c, 0:D], W2[rows, :]).then_inc(w_in, 16)
                sp.dma_start(w2_in[:, c, D:D + ER].rearrange("p (e r) -> p e r", r=R),
                             A2[:, rows, :].rearrange("e d r -> d e r")).then_inc(w_in, 16)
                sp.dma_start(w2_in[:, c, D + ER:YW], R2[rows, :]).then_inc(w_in, 16)
            sp.wait_ge(consts, 3)
            for k in range(3):
                sp.dma_start(b1_in[k * SB:k * SB + ER, :], B1.rearrange("e r h -> (e r) h")).then_inc(w_in, 16)
                sp.dma_start(b2_in[k * SB:k * SB + ER, :], B2.rearrange("e r h -> (e r) h")).then_inc(w_in, 16)
                sp.dma_start(b1_in[k * SB + ER:k * SB + ER + 1, :], b1.rearrange("(a n) -> a n", a=1)).then_inc(w_in, 16)
                sp.dma_start(b2_in[k * SB + ER:k * SB + ER + 1, :], b2.rearrange("(a n) -> a n", a=1)).then_inc(w_in, 16)
            for w, c0 in ((Wq, 0), (Wk, NH * FD), (Wv, 2 * NH * FD), (Wo, 2 * NH * FD + D)):
                sp.dma_start(aw_in[:, c0:c0 + w.shape[1]], w).then_inc(w_in, 16)
            for i in range(1, 4):
                sp.dma_start(xs[:, i * q:(i + 1) * q, :], xt[:, i * q:(i + 1) * q, :]).then_inc(x_in[i], 16)
            ot = out.rearrange("b l d -> (b l) d").rearrange("(t p) d -> p t d", p=P)
            for i in range(4):
                sp.wait_ge(ff2.done, (i + 1) * GROUPS // 4)
                sp.dma_start(ot[:, i * q:(i + 1) * q, :], xs[:, i * q:(i + 1) * q, :]).then_inc(stored, 16)
            sp.wait_ge(stored, 64)
        WEIGHT_DMAS = 3 + 3 * HC + 12 + 4

        @block.gpsimd
        def _(pool):
            pool.memset(b1_in[:, :], 0.0).then_inc(consts, 1)
            pool.memset(b2_in[:, :], 0.0).then_inc(consts, 1)
            pool.memset(m.neg_half[:, :], -0.5).then_inc(consts, 1)
            pool.memset(m.ident32[:, :], 0.0).then_inc(consts, 1)
            pool.memset(m.ident16[:, :], 0.0).then_inc(consts, 1)
            pool.memset(row_scale[:, :], 1.0 / R).then_inc(consts, 1)
            pool.wait_ge(consts, 6)
            for t in (m.ident32, m.ident16):
                pool.affine_select(out=t[:, :], in_=t[:, :], compare_op=ALU.not_equal, fill=1.0, base=0,
                                   pattern=[[-1, P]], channel_multiplier=1).then_inc(consts, 1)
            n = 8
            for k in range(3):
                for layer in range(2):
                    pool.wait_ge(consts, n)
                    pool.affine_select(out=row_scale[:, layer:layer + 1], in_=row_scale[:, layer:layer + 1],
                                       compare_op=ALU.not_equal, fill=WS ** (layer + 1), base=-(k * SB + ER),
                                       pattern=[[0, 1]], channel_multiplier=1).then_inc(consts, 1)
                    n += 1
            pool.memset(steps_in[:, 0:8:2], -1.0).then_inc(consts, 1)
            pool.memset(steps_in[:, 1:8:2], 1.0).then_inc(consts, 1)
            pool.memset(m.ones_tri[:, :], 1.0).then_inc(consts, 1)
            pool.wait_ge(consts, n + 3)
            pool.affine_select(out=steps_in[:, :], in_=steps_in[:, :], compare_op=ALU.is_ge, fill=0.0, base=-FD,
                               pattern=[[-FD, 8]], channel_multiplier=1).then_inc(consts, 1)
            pool.affine_select(out=m.ones_tri[:, :], in_=m.ones_tri[:, :], compare_op=ALU.is_ge, fill=0.0, base=0,
                               pattern=[[1, LEN]], channel_multiplier=-1).then_inc(consts, 1)
            ff1.gpsimd(pool)
            att.gpsimd(pool)
            ff2.gpsimd(pool)
        CONSTS = 19

        @block.vector
        def _(dve):
            for i in two:
                dve.memset(m.zs[i][:, :, :, :], 0.0).then_inc(prep, 1)
            dve.wait_ge(prep, 2)
            dve.memset(m.ve[:, :], 0.0).then_inc(m.started, 1)
            for i in two:
                dve.memset(m.zs[i][:, :, 0:3:2, ER:ER + 1], 1.0).then_inc(prep, 1)
            n = 4
            dve.wait_ge(prep, n)
            dve.wait_ge(consts, CONSTS)
            dve.wait_ge(w_in, 16 * WEIGHT_DMAS)
            for hi, lo, src in ((m.arh, m.arl, ar_in), (m.w1h, m.w1l, w1_in)):
                split(dve, hi[:, :], lo[:, :], src[:, :], WS, prep, n)
                n += 2
            split(dve, m.w2h[:, :, :], m.w2l[:, :, :], w2_in[:, :, :], WS, prep, n)
            n += 2
            for layer, (src, sc, st) in enumerate(((b1_in, b1_sc, m.b1s), (b2_in, b2_sc, m.b2s))):
                dve.tensor_scalar(sc[:, :], src[:, :], row_scale[:, layer:layer + 1], None, ALU.mult).then_inc(prep, 1)
                dve.wait_ge(prep, n + 1)
                dve.tensor_copy(st[:, :], sc[:, :]).then_inc(prep, 1)
                dve.wait_ge(prep, n + 2)
                lo = slice(2 * SB, SK)
                dve.tensor_tensor(st[lo, :], sc[lo, :], st[lo, :], ALU.subtract).then_inc(prep, 1)
                dve.wait_ge(prep, n + 3)
                n += 3
            for hi, lo, c0, signs in ((m.wqh, m.wql, 0, (WS, -WS)), (m.wkh, m.wkl, NH * FD, (WS, WS))):
                src = aw_in[:, c0:c0 + NH * FD].rearrange("p (h c) -> p h c", c=FD)
                for copy in two:
                    pair = [w[:, :].rearrange("p (h k c) -> p h k c", k=2, c=FD)[:, :, copy, :] for w in (hi, lo)]
                    split(dve, *pair, src, signs[copy], prep, n)
                    n += 2
            for hi, lo, c0 in ((m.wvh, m.wvl, 2 * NH * FD), (m.woh, m.wol, 2 * NH * FD + D)):
                split(dve, hi[:, :], lo[:, :], aw_in[:, c0:c0 + D], WS, prep, n)
                n += 2
            for v in (m.vf, m.vh, m.vl):
                dve.memset(v[:, :, :, :, :], 0.0).then_inc(prep, 1)
            n += 3
            dve.wait_ge(prep, n)
            for v in (m.vf, m.vh):
                dve.memset(v[:, :, :, :, HD:HD + 1], WS).then_inc(prep, 1)
            dve.tensor_reduce(m.lo_rows[:, :], steps_in[:, :], AX.X, ALU.add).then_inc(prep, 1)
            dve.wait_ge(prep, n + 3)
            dve.memset(m.ve[:, :], 0.0).then_inc(ready, 1)

            def x_ready(e, g):
                if isinstance(g, int):
                    e.wait_ge(x_in[g * 4 // GROUPS], 16)
                else:
                    for i in range(4):
                        e.wait_ge(x_in[i], 16)
            ff1.vector(dve, x_ready)
            dve.wait_ge(ff1.done, GROUPS)
            att.vector(dve)
            dve.wait_ge(att.done, BATCH)
            ff2.vector(dve, lambda e, g: None)

        @block.scalar
        def _(act):
            act.wait_ge(ready, 1)
            ff1.scalar(act)
            att.scalar(act)
            ff2.scalar(act)

        @block.tensor
        def _(pe):
            pe.wait_ge(ready, 1)
            pe.wait_ge(consts, CONSTS)
            ff1.tensor(pe)
            pe.wait_ge(ff1.done, GROUPS)
            att.tensor(pe)
            pe.wait_ge(att.done, BATCH)
            ff2.tensor(pe)


_INS = ["L0_attn_x", "L0_attn_Wq", "L0_attn_Wk", "L0_attn_Wv", "L0_attn_Wo", "L0_ffn_W1", "L0_ffn_b1", "L0_ffn_A1",
        "L0_ffn_B1", "L0_ffn_R1", "L0_ffn_W2", "L0_ffn_b2", "L0_ffn_A2", "L0_ffn_B2", "L0_ffn_R2"]


def kernel(**inputs):
    import numpy as np
    from concourse import bacc
    from concourse.bass_utils import run_bass_kernel_spmd

    nc = bacc.Bacc("TRN2", target_bir_lowering=False, num_devices=1)
    arrays, args = {}, []
    for name in _INS:
        a = np.ascontiguousarray(inputs[name])
        arrays[f"in_{name}"] = a
        args.append(nc.dram_tensor(f"in_{name}", a.shape, mybir.dt.from_np(a.dtype), kind="ExternalInput").ap())
    args.append(nc.dram_tensor("out_x", (BATCH, LEN, D), F32, kind="ExternalOutput").ap())
    program(nc, *args)
    return run_bass_kernel_spmd(nc, [arrays], core_ids=[0]).results[0]["out_x"]
```

```python
from contextlib import ExitStack

import concourse.bass as bass
from concourse import mybir

F32 = mybir.dt.float32
F16 = mybir.dt.float16
ALU = mybir.AluOpType
ACT = mybir.ActivationFunctionType
AX = mybir.AxisListType

P = 128
BATCH, LEN, D = 32, 256, 128
TILES = BATCH * LEN // P
GT = 4
GN = GT * P
GROUPS = TILES // GT
HID = 512
HC = HID // P
E, R = 3, 8
ER = E * R
YW = D + ER + E
ZW = ER + E
SB = 32
SK = 3 * SB
LN_EPS = 1e-5
WS = 4.0
GATE_LINKS = 6
FF_LEAD = 3
ATT_LEAD = 3
ST = LEN // P
NH, FD, HD = 16, 16, 8
SW = LEN + P
ATT_EPS = 1e-12


def split(e, hi, lo, src, scale, sem, base):
    e.tensor_scalar(hi, src, scale, None, ALU.mult).then_inc(sem, 1)
    e.wait_ge(sem, base + 1)
    e.scalar_tensor_tensor(out=lo, in0=src, scalar=scale, in1=hi, op0=ALU.mult, op1=ALU.subtract).then_inc(sem, 1)
    e.wait_ge(sem, base + 2)


def wait_alone(e, semaphore, value, started):
    if not isinstance(value, int):
        value = e.to_reg(value)
    e.wait_ge(started, 1)
    e.wait_ge(semaphore, value)


def exists(g, count):
    return not isinstance(g, int) or 0 <= g < count


def run_steps(e, step, count, lead, lag):
    pairs = (count - lead - 2) // 2
    for g in range(-lead, 2):
        step(g, g % 2)
    with e.Fori(1, 1 + pairs) as pair:
        step(2 * pair, 0)
        step(2 * pair + 1, 1)
    for g in range(2 + 2 * pairs, count + lag):
        step(g, g % 2)


class FeedForward:

    def __init__(self, nc, ctx, name, mem):
        sem = lambda what: ctx.enter_context(nc.semaphore(f"{name}_{what}"))
        self.m = mem
        self.stats = sem("stats")
        self.mean_var = sem("mean_var")
        self.pool_chain = sem("pool_chain")
        self.rstd = sem("rstd")
        self.xn = sem("xn")
        self.xT_ps = sem("xT_ps")
        self.xT_hi = sem("xT_hi")
        self.xT_lo = sem("xT_lo")
        self.z2_ps = sem("z2_ps")
        self.z1_ps = sem("z1_ps")
        self.logits = sem("logits")
        self.exps = sem("exps")
        self.gate_chain = sem("gate_chain")
        self.zs = sem("zs")
        self.zsT_ps = sem("zsT_ps")
        self.zsT2 = sem("zsT2")
        self.zsT1 = sem("zsT1")
        self.h_ps = sem("h_ps")
        self.h_hi = sem("h_hi")
        self.h_lo = sem("h_lo")
        self.y_ps = sem("y_ps")
        self.done = sem("done")

    @staticmethod
    def layers(g):
        return slice(0 if exists(g - 1, GROUPS) else 1, 2 if exists(g + 1, GROUPS) else 1)

    def vector(self, e, x_ready):
        m = self.m

        def stats(g, p, tiles):
            if tiles[0] == 0:
                x_ready(e, g)
            for t in tiles:
                last = e.bn_stats(m.bn[:, p, t, :], m.x[:, bass.ds(g * GN + t * P, P)])
            if tiles[-1] == GT - 1:
                last.then_inc(self.stats, 1)

        def mean_var(g, p):
            wait_alone(e, self.stats, g + 1, m.started)
            for t in range(GT):
                last = e.bn_aggr(m.mv[:, p, t, :], m.bn[:, p, t, :])
            last.then_inc(self.mean_var, 1)

        def xT_lo(g, p):
            e.wait_ge(self.xT_hi, g + 1)
            e.tensor_tensor(m.xl[:, p, :], m.psT[:, :], m.xh[:, p, :], ALU.subtract).then_inc(self.xT_lo, 1)

        def gates(g, p):
            of, n = self.layers(g), [0]
            width = of.stop - of.start

            def link(ins):
                n[0] += 1
                ins.then_inc(self.gate_chain, 1)
                e.wait_ge(self.gate_chain, (g + 1) * GATE_LINKS + n[0])

            if of.start == 0:
                e.wait_ge(self.z2_ps, g)
            if of.stop == 2:
                e.wait_ge(self.z1_ps, g + 2)
            logits, mx, lg, sm = m.psR[:, :, of, ER:ZW], m.mx[:, :, of], m.lg[:, :, of, :], m.sm[:, :, of]
            ex, gt = m.ex[:, :, of, :], m.gt[:, :, of, :]
            link(e.tensor_reduce(mx, logits, AX.X, ALU.max))
            e.tensor_tensor(lg, logits, mx.unsqueeze(3).broadcast_to([P, GT, width, E]),
                            ALU.subtract).then_inc(self.logits, 1)
            if exists(g + 3, GROUPS):
                stats(g + 3, 1 - p, (0, 1))
            e.wait_ge(self.exps, g + 2)
            link(e.tensor_reduce(sm, ex, AX.X, ALU.add))
            link(e.reciprocal(sm, sm))
            link(e.tensor_tensor(gt, ex, sm.unsqueeze(3).broadcast_to([P, GT, width, E]), ALU.mult))
            for i in range(of.start, of.stop):
                last = e.tensor_tensor(m.zg[:, :, i, :].rearrange("p t (e r) -> p t e r", r=R),
                                       m.psR[:, :, i, 0:ER].rearrange("p t (e r) -> p t e r", r=R),
                                       m.gt[:, :, i, :].unsqueeze(3).broadcast_to([P, GT, E, R]), ALU.mult)
            link(last)
            for i in range(of.start, of.stop):
                last = e.tensor_copy(m.zs[:, :, i, 0:3:2, 0:ER],
                                     m.zg[:, :, i, :].unsqueeze(2).broadcast_to([P, GT, 2, ER]))
            link(last)
            e.tensor_tensor(m.zs[:, :, of, 1, 0:ER], m.zg[:, :, of, :], m.zs[:, :, of, 0, 0:ER],
                            ALU.subtract).then_inc(self.zs, 1)

        def h_lo(g, pair):
            e.wait_ge(self.h_hi, 2 * g + pair + 1)
            e.scalar_tensor_tensor(out=m.hl[:, 2 * pair:2 * pair + 2, :], in0=m.psH[pair][:, :, :], scalar=0.0,
                                   in1=m.hh[:, 2 * pair:2 * pair + 2, :], op0=ALU.max,
                                   op1=ALU.subtract).then_inc(self.h_lo, 1)

        def residual(g):
            e.wait_ge(self.y_ps, g + 1)
            for half in range(2):
                xg = m.x[:, bass.ds(g * GN + half * 2 * P, 2 * P)].rearrange("p (t d) -> p t d", d=D)
                e.scalar_tensor_tensor(out=xg, in0=m.psY[:, half, :, 0:D], scalar=0.5 / (WS * WS), in1=xg,
                                       op0=ALU.mult, op1=ALU.add).then_inc(self.done, 1)

        def step(g, p):
            if exists(g - 1, GROUPS) or exists(g + 1, GROUPS):
                gates(g, p)
            elif exists(g + 3, GROUPS):
                stats(g + 3, 1 - p, (0, 1))
            if exists(g, GROUPS):
                h_lo(g, 0)
            if exists(g + 3, GROUPS):
                stats(g + 3, 1 - p, (2, 3))
            if exists(g - 1, GROUPS):
                residual(g - 1)
            if exists(g + 3, GROUPS):
                mean_var(g + 3, 1 - p)
            if exists(g, GROUPS):
                h_lo(g, 1)
            if exists(g + 2, GROUPS):
                xT_lo(g + 2, p)
        run_steps(e, step, GROUPS, FF_LEAD, 1)

    def scalar(self, e):
        m = self.m

        def norm(g, p):
            e.wait_ge(self.rstd, g + 1)
            for t in range(GT):
                last = e.activation(m.xn[:, t, :], m.x[:, bass.ds(g * GN + t * P, P)], ACT.Identity,
                                    bias=m.nm[:, p, t:t + 1], scale=m.rs[:, p, t:t + 1])
            last.then_inc(self.xn, 1)

        def xT_hi(g, p):
            e.wait_ge(self.xT_ps, g + 1)
            e.activation(m.xh[:, p, :], m.psT[:, :], ACT.Copy).then_inc(self.xT_hi, 1)

        def exps(g):
            of = self.layers(g)
            e.wait_ge(self.logits, g + 2)
            e.activation(m.ex[:, :, of, :], m.lg[:, :, of, :], ACT.Exp, scale=WS ** -2).then_inc(self.exps, 1)

        def zsT2(g):
            e.wait_ge(self.zsT_ps, g + 3)
            e.activation(m.zsT2[:, :], m.psZT[0:SK, 0:GN], ACT.Copy).then_inc(self.zsT2, 1)

        def zsT1(g, p):
            e.wait_ge(self.zsT_ps, g + 1)
            e.activation(m.zsT1[:, p, :], m.psZT[0:SK, GN:2 * GN], ACT.Copy).then_inc(self.zsT1, 1)

        def h_hi(g, pair):
            e.wait_ge(self.h_ps, 2 * g + pair + 1)
            e.activation(m.hh[:, 2 * pair:2 * pair + 2, :], m.psH[pair][:, :, :], ACT.Relu).then_inc(self.h_hi, 1)

        def step(g, p):
            if exists(g - 1, GROUPS) or exists(g + 1, GROUPS):
                exps(g)
            if exists(g, GROUPS):
                h_hi(g, 0)
            if exists(g - 1, GROUPS):
                zsT2(g - 1)
            if exists(g + 1, GROUPS):
                zsT1(g + 1, 1 - p)
            if exists(g, GROUPS):
                h_hi(g, 1)
            if exists(g + 2, GROUPS):
                xT_hi(g + 2, p)
            if exists(g + 3, GROUPS):
                norm(g + 3, 1 - p)
        run_steps(e, step, GROUPS, FF_LEAD, 1)

    def gpsimd(self, e):
        m = self.m

        def rstd(g, p):
            wait_alone(e, self.mean_var, g + 1, m.started)
            e.tensor_scalar(m.ve[:, 0:GT], m.mv[:, p, :, 1], LN_EPS, None, ALU.add)
            e.tensor_scalar(m.nm[:, p, :], m.mv[:, p, :, 0], -1.0, None, ALU.mult).then_inc(self.pool_chain, 1)
            e.wait_ge(self.pool_chain, 2 * g + 1)
            e.tensor_tensor(m.rs[:, p, :], m.ve[:, 0:GT], m.neg_half[:, 0:GT], ALU.pow).then_inc(self.pool_chain, 1)
            e.wait_ge(self.pool_chain, 2 * g + 2)
            e.tensor_tensor(m.nm[:, p, :], m.nm[:, p, :], m.rs[:, p, :], ALU.mult).then_inc(self.rstd, 1)

        def step(g, p):
            if exists(g + 3, GROUPS):
                rstd(g + 3, 1 - p)
        run_steps(e, step, GROUPS, FF_LEAD, 1)

    def tensor(self, e):
        m = self.m

        def mm(out, lhsT, rhs, start, stop):
            return e.matmul(out, lhsT, rhs, start=start, stop=stop, skip_group_check=True)

        def xT(g):
            e.wait_ge(self.xn, g + 1)
            if not (isinstance(g, int) and g == 0):
                e.wait_ge(self.xT_lo, g)
            for t in range(GT):
                last = e.transpose(m.psT[:, t * P:(t + 1) * P], m.xn[:, t, :], m.ident32[:, :])
            last.then_inc(self.xT_ps, 1)

        def z1(g, p, opens):
            if opens and g > 0:
                e.wait_ge(self.zs, g)
            for t in range(GT):
                out, tok = m.psR[:, t, 1, 0:ZW], slice(t * P, (t + 1) * P)
                e.wait_ge(self.xT_hi, g + 1)
                mm(out, m.xh[:, p, tok], m.arh[:, :], opens and t % 2 == 0, False)
                mm(out, m.xh[:, p, tok], m.arl[:, :], False, False)
                e.wait_ge(self.xT_lo, g + 1)
                last = mm(out, m.xl[:, p, tok], m.arh[:, :], False, True)
            last.then_inc(self.z1_ps, 1)

        def zsT(g):
            of = self.layers(g)
            e.wait_ge(self.zs, g + 2)
            for i in range(of.start, of.stop):
                for t in range(GT):
                    last = e.transpose(m.psZT[0:SK, i * GN + t * P:i * GN + (t + 1) * P],
                                       m.zs[:, t, i, :, :].rearrange("p k c -> p (k c)"), m.ident16[:, :])
            last.then_inc(self.zsT_ps, 1)

        def hidden(g, p, chunks):
            pair = chunks[0] // 2
            if chunks[0] % 2 == 0:
                if not (isinstance(g, int) and g == 0):
                    e.wait_ge(self.h_lo, 2 * (g - 1) + pair + 1)
                e.wait_ge(self.zsT1, g + 1)
            for c in chunks:
                cols, out = slice(c * P, (c + 1) * P), m.psH[pair][:, c % 2, :]
                mm(out, m.w1h[:, cols], m.xh[:, p, :], True, False)
                mm(out, m.w1l[:, cols], m.xh[:, p, :], False, False)
                mm(out, m.w1h[:, cols], m.xl[:, p, :], False, False)
                last = mm(out, m.b1s[:, cols], m.zsT1[:, p, :], False, True)
            if chunks[-1] % 2 == 1:
                last.then_inc(self.h_ps, 1)

        def second(g, pair):
            e.wait_ge(self.h_lo, 2 * g + pair + 1)
            for half in range(2):
                if pair == 0 and not (isinstance(g, int) and g == 0):
                    e.wait_ge(self.done, 2 * g - 1 + half)
                for c in (2 * pair, 2 * pair + 1):
                    for t in (2 * half, 2 * half + 1):
                        out, tok = m.psY[:, half, t % 2, 0:YW], slice(t * P, (t + 1) * P)
                        mm(out, m.hh[:, c, tok], m.w2h[:, c, :], c == 0 and t % 2 == 0, False)
                        mm(out, m.hh[:, c, tok], m.w2l[:, c, :], False, False)
                        last = mm(out, m.hl[:, c, tok], m.w2h[:, c, :], False, c == HC - 1)
            if pair == 1:
                last.then_inc(self.z2_ps, 1)

        def adapters2(g):
            e.wait_ge(self.zsT2, g + 1)
            for t in range(GT):
                last = mm(m.psY[:, t // 2, t % 2, 0:D], m.zsT2[:, t * P:(t + 1) * P], m.b2s[:, :], False, True)
            last.then_inc(self.y_ps, 1)

        def step(g, p):
            if exists(g, GROUPS):
                hidden(g, p, (0, 1))
                hidden(g, p, (2,))
            if exists(g - 1, GROUPS) or exists(g + 1, GROUPS):
                zsT(g)
            if exists(g, GROUPS):
                hidden(g, p, (3,))
            if exists(g - 1, GROUPS):
                adapters2(g - 1)
            if exists(g + 2, GROUPS):
                xT(g + 2)
            if exists(g, GROUPS):
                second(g, 0)
                second(g, 1)
            if exists(g + 2, GROUPS):
                z1(g + 2, p, opens=not exists(g, GROUPS))
        run_steps(e, step, GROUPS, FF_LEAD, 1)


class Attention:

    def __init__(self, nc, ctx, name, mem):
        sem = lambda what: ctx.enter_context(nc.semaphore(f"{name}_{what}"))
        self.m = mem
        self.stats = sem("stats")
        self.mean_var = sem("mean_var")
        self.pool_chain = sem("pool_chain")
        self.rstd = sem("rstd")
        self.xn = sem("xn")
        self.xT_ps = sem("xT_ps")
        self.xT_hi = sem("xT_hi")
        self.xT_lo = sem("xT_lo")
        self.qk_ps = sem("qk_ps")
        self.qk_hi = sem("qk_hi")
        self.qk_lo = sem("qk_lo")
        self.hi_again = sem("hi_again")
        self.stack_ps = sem("stack_ps")
        self.stacks = sem("stacks")
        self.v_ps = sem("v_ps")
        self.v_hi = sem("v_hi")
        self.v_lo = sem("v_lo")
        self.s_ps = sem("s_ps")
        self.squares = sem("squares")
        self.masked = sem("masked")
        self.sums_ps = sem("sums_ps")
        self.sums = sem("sums")
        self.ytok_ps = sem("ytok_ps")
        self.y_chain = sem("y_chain")
        self.y = sem("y")
        self.yT_ps = sem("yT_ps")
        self.yT_hi = sem("yT_hi")
        self.yT_lo = sem("yT_lo")
        self.out_ps = sem("out_ps")
        self.done = sem("done")

    def vector(self, e):
        m = self.m

        def tile(b, t):
            return m.x[:, bass.ds(b * LEN + t * P, P)]

        def stats(b):
            for t in range(ST):
                last = e.bn_stats(m.bn[:, 0, t, :], tile(b, t))
            last.then_inc(self.stats, 1)

        def mean_var(b):
            wait_alone(e, self.stats, b + 1, m.started)
            for t in range(ST):
                last = e.bn_aggr(m.mv[:, 0, t, :], m.bn[:, 0, t, :])
            last.then_inc(self.mean_var, 1)

        def norm(b):
            e.wait_ge(self.rstd, b + 1)
            if not (isinstance(b, int) and b == 0):
                e.wait_ge(self.xT_ps, b)
            for t in range(ST):
                last = e.tensor_scalar(m.xn[:, t, :], tile(b, t), m.mv[:, 0, t, 0:1], m.rs[:, 0, t:t + 1],
                                       ALU.subtract, ALU.mult)
            last.then_inc(self.xn, 1)

        def xT_lo(b, p):
            e.wait_ge(self.xT_hi, b + 1)
            e.tensor_tensor(m.axl[:, p, :], m.psT[:, 0:LEN], m.axh[:, p, :], ALU.subtract).then_inc(self.xT_lo, 1)

        def qk_lo(b, which):
            e.wait_ge(self.qk_hi, 2 * b + 2)
            e.tensor_tensor(m.qk[:, :, which, :, 1 + which, :], m.psQK[:, :, which, :, :],
                            m.qk[:, :, which, :, 0, :], ALU.subtract).then_inc(self.qk_lo, 1)

        def hi_again(b, which):
            e.wait_ge(self.qk_hi, 2 * b + 2)
            e.tensor_copy(m.qk[:, :, which, :, 2 - which, :], m.qk[:, :, which, :, 0, :]).then_inc(self.hi_again, 1)

        def stack(b, p, which, half):
            e.wait_ge(self.stack_ps, 4 * b + 2 * which + half + 1)
            us = slice(4 * half, 4 * half + 4)
            e.tensor_copy(m.stack[which][:, p, us, :], m.psSt[:, us, :]).then_inc(self.stacks, 1)

        def v_lo(b, p):
            e.wait_ge(self.v_hi, b + 1)
            e.tensor_tensor(m.vl[:, p, :, :, 0:HD], m.psV, m.vh[:, p, :, :, 0:HD], ALU.subtract).then_inc(self.v_lo, 1)

        def normalise(b):
            n = b * 2
            e.wait_ge(self.ytok_ps, b + 1)
            e.tensor_scalar(m.den[:, :, :], m.psYt[:, :, :, HD], 2 * WS * ATT_EPS, None, ALU.add).then_inc(self.y_chain, 1)
            e.wait_ge(self.y_chain, n + 1)
            e.reciprocal(m.den[:, :, :], m.den[:, :, :]).then_inc(self.y_chain, 1)
            e.wait_ge(self.y_chain, n + 2)
            e.tensor_tensor(m.yn[:, :, :, :], m.psYt[:, :, :, 0:HD],
                            m.den[:, :, :].unsqueeze(3).broadcast_to([P, ST, NH, HD]), ALU.mult).then_inc(self.y, 1)

        def yT_lo(b):
            e.wait_ge(self.yT_hi, b + 1)
            e.tensor_tensor(m.yl[:, :], m.psT[:, 0:LEN], m.yh[:, :], ALU.subtract).then_inc(self.yT_lo, 1)

        def residual(b):
            e.wait_ge(self.out_ps, b + 1)
            xb = m.x[:, bass.ds(b * LEN, LEN)]
            e.scalar_tensor_tensor(out=xb, in0=m.psT[:, LEN:2 * LEN], scalar=1.0 / WS, in1=xb, op0=ALU.mult,
                                   op1=ALU.add).then_inc(self.done, 1)

        def step(b, p):
            prev, nxt, nxt2, nxt3 = (exists(b + k, BATCH) for k in (-1, 1, 2, 3))
            if nxt3:
                stats(b + 3)
            if nxt2:
                xT_lo(b + 2, p)
            if nxt3:
                mean_var(b + 3)
            if prev:
                normalise(b - 1)
            if nxt:
                v_lo(b + 1, 1 - p)
                stack(b + 1, 1 - p, 0, 0)
                stack(b + 1, 1 - p, 0, 1)
            if prev:
                yT_lo(b - 1)
            if nxt:
                stack(b + 1, 1 - p, 1, 0)
            if nxt3:
                norm(b + 3)
            if nxt:
                stack(b + 1, 1 - p, 1, 1)
            if prev:
                residual(b - 1)
            if nxt2:
                qk_lo(b + 2, 0)
                qk_lo(b + 2, 1)
                hi_again(b + 2, 0)
                hi_again(b + 2, 1)
        run_steps(e, step, BATCH, ATT_LEAD, 1)

    def scalar(self, e):
        m = self.m

        def square(b, k, first):
            e.wait_ge(self.s_ps, 8 * b + k + 1)
            if not first:
                e.wait_ge(self.sums_ps, 4 * (b - 1) + k // 2 + 1)
            e.activation(m.G[:, k, :, :], m.psS[k % 2][:, :, 0:SW], ACT.Square, bias=1.0,
                         scale=0.25 / (WS * WS)).then_inc(self.squares, 1)

        def sums(b, half):
            e.wait_ge(self.sums_ps, 4 * b + 2 * half + 2)
            e.activation(m.YT[:, 2 * half:2 * half + 2, :], m.psU, ACT.Copy).then_inc(self.sums, 1)

        def xT_hi(b, p):
            e.wait_ge(self.xT_ps, b + 1)
            e.activation(m.axh[:, p, :], m.psT[:, 0:LEN], ACT.Copy).then_inc(self.xT_hi, 1)

        def v_hi(b, p):
            e.wait_ge(self.v_ps, b + 1)
            e.activation(m.vf[:, p, :, :, 0:HD], m.psV, ACT.Copy)
            e.activation(m.vh[:, p, :, :, 0:HD], m.psV, ACT.Copy).then_inc(self.v_hi, 1)

        def qk_hi(b, t):
            e.wait_ge(self.qk_ps, 2 * b + t + 1)
            e.activation(m.qk[:, t, :, :, 0, :], m.psQK[:, t, :, :, :], ACT.Copy).then_inc(self.qk_hi, 1)

        def yT_hi(b):
            e.wait_ge(self.yT_ps, b + 1)
            e.activation(m.yh[:, :], m.psT[:, 0:LEN], ACT.Copy).then_inc(self.yT_hi, 1)

        def step(b, p):
            prev, main, nxt, nxt2 = (exists(b + k, BATCH) for k in (-1, 0, 1, 2))
            zero = isinstance(b, int) and b == 0
            if main:
                square(b, 0, zero)
                square(b, 1, zero)
            if prev:
                sums(b - 1, 1)
            if nxt2:
                xT_hi(b + 2, p)
            if main:
                square(b, 2, zero)
                square(b, 3, zero)
            if nxt:
                v_hi(b + 1, 1 - p)
            if main:
                square(b, 4, zero)
                square(b, 5, zero)
                sums(b, 0)
            if prev:
                yT_hi(b - 1)
            if main:
                square(b, 6, zero)
                square(b, 7, zero)
            if nxt2:
                qk_hi(b + 2, 0)
                qk_hi(b + 2, 1)
        run_steps(e, step, BATCH, ATT_LEAD, 1)

    def gpsimd(self, e):
        m = self.m

        def rstd(b):
            wait_alone(e, self.mean_var, b + 1, m.started)
            e.tensor_scalar(m.ve[:, 0:ST], m.mv[:, 0, 0:ST, 1], LN_EPS, None, ALU.add).then_inc(self.pool_chain, 1)
            e.wait_ge(self.pool_chain, b + 1)
            e.tensor_tensor(m.rs[:, 0, 0:ST], m.ve[:, 0:ST], m.neg_half[:, 0:ST], ALU.pow).then_inc(self.rstd, 1)

        def mask(b, k):
            wait_alone(e, self.squares, 8 * b + k + 1, m.started)
            for h in range(2):
                g = m.G[:, k, h, :].rearrange("p (c n) -> p c n", n=P)[:, 0:3:2, :]
                last = e.affine_select(out=g, in_=g, compare_op=ALU.is_ge, fill=0.0, base=0,
                                       pattern=[[0, 2], [1, P]], channel_multiplier=-1)
            last.then_inc(self.masked, 1)

        def step(b, p):
            main = exists(b, BATCH)
            if main:
                for k in range(4):
                    mask(b, k)
            if exists(b + 3, BATCH):
                rstd(b + 3)
            if main:
                for k in range(4, NH // 2):
                    mask(b, k)
        run_steps(e, step, BATCH, ATT_LEAD, 1)

    def tensor(self, e):
        m = self.m

        def mm(out, lhsT, rhs, start, stop, **kw):
            return e.matmul(out, lhsT, rhs, start=start, stop=stop, skip_group_check=True, **kw)


        def xT(b, free):
            e.wait_ge(self.xn, b + 1)
            if free:
                e.wait_ge(self.done, b - 3)
            for t in range(ST):
                last = e.transpose(m.psT[:, t * P:(t + 1) * P], m.xn[:, t, :], m.ident32[:, :])
            last.then_inc(self.xT_ps, 1)

        def v(b, p, tokens, free):
            e.wait_ge(self.xT_lo, b + 2 if tokens else b + 1)
            if free:
                e.wait_ge(self.done, b - 2)
            for t in range(ST):
                out, tok = m.psT[:, LEN + t * P:LEN + (t + 1) * P], slice(t * P, (t + 1) * P)
                mm(out, m.axh[:, p, tok], m.wvh[:, :], t == 0, False)
                mm(out, m.axh[:, p, tok], m.wvl[:, :], False, False)
                last = mm(out, m.axl[:, p, tok], m.wvh[:, :], False, True)
            last.then_inc(self.v_ps, 1)

        def project(b, p, t, stacks):
            e.wait_ge(self.xT_lo, b + 1)
            if stacks:
                e.wait_ge(self.stacks, 4 * (b - 1) + t + 3)
            out, tok = m.psH[0][:, t, :], slice(t * P, (t + 1) * P)
            mm(out, m.axh[:, p, tok], m.wqkh[:, :], True, False)
            mm(out, m.axh[:, p, tok], m.wqkl[:, :], False, False)
            mm(out, m.axl[:, p, tok], m.wqkh[:, :], False, True).then_inc(self.qk_ps, 1)

        def stack(b, which, half):
            if which == 0:
                e.wait_ge(self.qk_lo, 2 * b + 2)
                e.wait_ge(self.hi_again, 2 * b + 2)
            else:
                e.wait_ge(self.stacks, 4 * b + half + 1)
            for u in range(4 * half, 4 * half + 4):
                for t in range(ST):
                    rows = m.qk[:, t, which, 2 * u:2 * u + 2, :, :].rearrange("p h k c -> p (h k c)")
                    last = e.transpose(m.psSt[:, u, t * P:(t + 1) * P], rows, m.ident16[:, :])
            last.then_inc(self.stack_ps, 1)

        def scores(b, p, k, first):
            if k >= 2 or not first:
                e.wait_ge(self.squares, 8 * b + k - 1)
            if k % 4 == 0:
                e.wait_ge(self.stacks, 4 * b + 3 + k // 4)
            for h in range(2):
                rows = slice(64 * h, 64 * h + 64)
                for kt, (n0, c0) in enumerate(((0, 0), (P, LEN))):
                    last = mm(m.psS[k % 2][:, h, c0:c0 + LEN - n0], m.stack[1][rows, p, k, kt * P:(kt + 1) * P],
                              m.stack[0][rows, p, k, n0:LEN], kt == 0, kt == 1, tile_position=(64 * h, 0))
            last.then_inc(self.s_ps, 1)

        def head_sums(b, p, j, free):
            e.wait_ge(self.masked, 8 * b + 2 * j + 2)
            if j == 0:
                e.wait_ge(self.v_lo, b + 1)
                if free:
                    e.wait_ge(self.sums, 2 * b)
            if j == 2:
                e.wait_ge(self.sums, 2 * b + 1)
            out = m.psU[:, j % 2, :]
            for kt, n0, c0 in ((0, 0, 0), (1, P, LEN)):
                for i in range(4):
                    last = mm(out[32 * i:32 * i + 32, n0:LEN], m.vf[:, p, kt, 4 * j + i, :],
                              m.G[:, 2 * j + i // 2, i % 2, c0:c0 + LEN - n0], kt == 0, kt == 1,
                              tile_position=(0, 32 * i))
            last.then_inc(self.sums_ps, 1)

        def ytok(b, p, projected, stacked):
            e.wait_ge(self.sums, 2 * b + 2)
            if projected:
                e.wait_ge(self.qk_lo, 2 * b + 6)
            elif stacked:
                e.wait_ge(self.stacks, 4 * b + 8)
            for t in range(ST):
                for j in range(4):
                    mm(m.psYf[:, t, j, :], m.YT[:, j, t * P:(t + 1) * P], m.ident32[:, :], j == 0, False,
                       is_transpose=True)
                for kt in range(t + 1):
                    upto = m.ones_tri[:, (t - kt) * P:(t - kt + 1) * P]
                    for vv in (m.vh, m.vl):
                        last = mm(m.psYt[:, t, :, 0:HD + 1], upto, vv[:, p, kt, :, 0:HD + 1], False, kt == t)
            last.then_inc(self.ytok_ps, 1)

        def yT(b, v_there):
            e.wait_ge(self.y, b + 1)
            if v_there:
                e.wait_ge(self.v_lo, b + 3)
            for t in range(ST):
                last = e.transpose(m.psT[:, t * P:(t + 1) * P], m.yn[:, t, :, :].rearrange("p h c -> p (h c)"),
                                   m.ident32[:, :])
            last.then_inc(self.yT_ps, 1)

        def output(b):
            e.wait_ge(self.yT_lo, b + 1)
            for t in range(ST):
                out, tok = m.psT[:, LEN + t * P:LEN + (t + 1) * P], slice(t * P, (t + 1) * P)
                mm(out, m.yh[:, tok], m.woh[:, :], t == 0, False)
                mm(out, m.yh[:, tok], m.wol[:, :], False, False)
                last = mm(out, m.yl[:, tok], m.woh[:, :], False, True)
            last.then_inc(self.out_ps, 1)

        def step(b, p):
            prev, main, nxt, nxt2 = (exists(b + k, BATCH) for k in (-1, 0, 1, 2))
            zero = isinstance(b, int) and b == 0
            if main:
                scores(b, p, 0, zero)
                scores(b, p, 1, zero)
            if prev:
                head_sums(b - 1, 1 - p, 3, True)
            if main:
                scores(b, p, 2, zero)
            if nxt2:
                xT(b + 2, not (isinstance(b, int) and b < 2))
            if main:
                scores(b, p, 3, zero)
            if prev:
                ytok(b - 1, 1 - p, nxt, main)
            if main:
                head_sums(b, p, 0, not zero)
            if nxt:
                v(b + 1, 1 - p, nxt2, not (isinstance(b, int) and b < 2))
            if main:
                scores(b, p, 4, zero)
            if nxt:
                if prev:
                    e.wait_ge(self.y, b)
                stack(b + 1, 0, 0)
                stack(b + 1, 0, 1)
            if main:
                scores(b, p, 5, zero)
                head_sums(b, p, 1, not zero)
            if prev:
                yT(b - 1, nxt)
            if nxt:
                stack(b + 1, 1, 0)
                stack(b + 1, 1, 1)
            if main:
                scores(b, p, 6, zero)
                scores(b, p, 7, zero)
                head_sums(b, p, 2, not zero)
            if nxt2:
                project(b + 2, p, 0, nxt)
                project(b + 2, p, 1, nxt)
            if prev:
                output(b - 1)
        run_steps(e, step, BATCH, ATT_LEAD, 1)


class Memory:
    pass


def program(nc, x, Wq, Wk, Wv, Wo, W1, b1, A1, B1, R1, W2, b2, A2, B2, R2, out):
    with ExitStack() as ctx:
        m = Memory()

        def sb(name, shape, dt):
            return ctx.enter_context(nc.sbuf_tensor(name, shape, dt))

        def ps(name, shape, dt=F32):
            return ctx.enter_context(nc.psum_tensor(name, shape, dt))

        def sem(name):
            return ctx.enter_context(nc.semaphore(name))

        m.x = sb("x_sb", [P, TILES * D], F32)
        w1_in = sb("w1_in", [P, HID], F32)
        ar_in = sb("ar_in", [P, ZW], F32)
        w2_in = sb("w2_in", [P, HC, YW], F32)
        b1_in = sb("b1_in", [SK, HID], F32)
        b2_in = sb("b2_in", [SK, D], F32)
        row_scale = sb("row_scale", [SK, 2], F32)
        b1_sc = sb("b1_sc", [SK, HID], F32)
        b2_sc = sb("b2_sc", [SK, D], F32)
        m.w1h, m.w1l = sb("w1h", [P, HID], F16), sb("w1l", [P, HID], F16)
        m.arh, m.arl = sb("arh", [P, ZW], F16), sb("arl", [P, ZW], F16)
        m.w2h, m.w2l = sb("w2h", [P, HC, YW], F16), sb("w2l", [P, HC, YW], F16)
        m.b1s, m.b2s = sb("b1s", [SK, HID], F16), sb("b2s", [SK, D], F16)
        m.ident32, m.ident16 = sb("ident32", [P, P], F32), sb("ident16", [P, P], F16)
        m.neg_half = sb("neg_half", [P, GT], F32)
        m.bn = sb("bn", [P, 2, GT, 6], F32)
        m.mv = sb("mv", [P, 2, GT, 2], F32)
        m.ve = sb("ve", [P, GT], F32)
        m.rs = sb("rs", [P, 2, GT], F32)
        m.nm = sb("nm", [P, 2, GT], F32)
        m.xn = sb("xn", [P, GT, D], F32)
        m.xh, m.xl = sb("xh", [P, 2, GN], F16), sb("xl", [P, 2, GN], F16)
        two = range(2)
        m.mx = sb("mx", [P, GT, 2], F32)
        m.lg = sb("lg", [P, GT, 2, E], F32)
        m.ex = sb("ex", [P, GT, 2, E], F32)
        m.sm = sb("sm", [P, GT, 2], F32)
        m.gt = sb("gt", [P, GT, 2, E], F32)
        m.zg = sb("zg", [P, GT, 2, ER], F32)
        m.zs = sb("zs", [P, GT, 2, 3, SB], F16)
        m.zsT2 = sb("zsT2", [SK, GN], F16)
        m.zsT1 = sb("zsT1", [SK, 2, GN], F16)
        m.hh, m.hl = sb("hh", [P, HC, GN], F16), sb("hl", [P, HC, GN], F16)

        aw_in = sb("aw_in", [P, 2 * NH * FD + 2 * D], F32)
        m.wqkh, m.wqkl = sb("wqkh", [P, 2 * NH * FD], F16), sb("wqkl", [P, 2 * NH * FD], F16)
        m.wvh, m.wvl = sb("wvh", [P, D], F16), sb("wvl", [P, D], F16)
        m.woh, m.wol = sb("woh", [P, D], F16), sb("wol", [P, D], F16)
        m.ones_tri = sb("ones_tri", [P, LEN], F16)
        m.axh, m.axl = sb("axh", [P, 2, LEN], F16), sb("axl", [P, 2, LEN], F16)
        m.qk = sb("qk", [P, ST, 2, NH, 4, FD], F16)
        m.stack = [sb(n, [P, 2, NH // 2, LEN], F16) for n in ("q_stack", "k_stack")]
        m.vf = sb("vf", [P, 2, ST, NH, 32], F32)
        m.vh, m.vl = sb("vh", [P, 2, ST, NH, 32], F16), sb("vl", [P, 2, ST, NH, 32], F16)
        m.G = sb("G", [P, NH // 2, 2, SW], F32)
        m.YT = sb("YT", [P, 4, LEN], F32)
        m.den = sb("den", [P, ST, NH], F32)
        m.yn = sb("yn", [P, ST, NH, HD], F32)
        m.yh, m.yl = sb("yh", [P, LEN], F16), sb("yl", [P, LEN], F16)

        m.psH = [ps(f"psH{i}", [P, 2, GN]) for i in two]
        m.psY = ps("psY", [P, 2, 2, 2 * P])
        m.psT = ps("psT", [P, GN])
        bank = ps("psB", [P, GN])
        m.psR = m.psY[:, :, :, :].rearrange("p a b n -> p (a b) n")[:, :, D:D + 2 * SB].rearrange(
            "p t (i c) -> p t i c", c=SB)
        m.psZT = bank[:, :].bitcast(F16)
        m.psQK = m.psH[0][:, :, :].rearrange("p t (w h c) -> p t w h c", w=2, c=FD)
        m.psSt = m.psH[0][:, :, :].rearrange("p a n -> p (a n)").bitcast(F16).rearrange("p (u n) -> p u n", n=LEN)
        m.psYf = m.psH[0][:, :, :].rearrange("p t (j c) -> p t j c", c=P)
        m.psYt = m.psH[0][:, :, :].rearrange("p t (h c) -> p t h c", c=32)
        m.psS = [m.psH[1][:, :, :], m.psY[:, :, :, :].rearrange("p a b n -> p a (b n)")]
        m.psV = m.psT[:, LEN:2 * LEN].rearrange("p (t h c) -> p t h c", h=NH, c=HD)
        m.psU = bank[:, :].rearrange("p (j n) -> p j n", n=LEN)

        w_in = sem("w_in")
        x_in = [sem(f"x_in{i}") for i in range(4)]
        consts = sem("consts")
        m.started = sem("started")
        prep = sem("prep")
        ready = sem("ready")
        stored = sem("stored")
        ff1 = FeedForward(nc, ctx, "ff1", m)
        att = Attention(nc, ctx, "att", m)
        ff2 = FeedForward(nc, ctx, "ff2", m)

        block = ctx.enter_context(nc.Block())

        @block.sync
        def _(sp):
            xt = x.rearrange("b l d -> (b l) d").rearrange("(t p) d -> p t d", p=P)
            xs = m.x[:, :].rearrange("p (t d) -> p t d", d=D)
            q = TILES // 4
            sp.dma_start(xs[:, 0:q, :], xt[:, 0:q, :]).then_inc(x_in[0], 16)
            sp.dma_start(w1_in[:, :], W1).then_inc(w_in, 16)
            sp.dma_start(ar_in[:, 0:ER].rearrange("p (e r) -> p e r", r=R), A1.rearrange("e d r -> d e r")).then_inc(w_in, 16)
            sp.dma_start(ar_in[:, ER:ZW], R1).then_inc(w_in, 16)
            for c in range(HC):
                rows = slice(c * P, (c + 1) * P)
                sp.dma_start(w2_in[:, c, 0:D], W2[rows, :]).then_inc(w_in, 16)
                sp.dma_start(w2_in[:, c, D:D + ER].rearrange("p (e r) -> p e r", r=R),
                             A2[:, rows, :].rearrange("e d r -> d e r")).then_inc(w_in, 16)
                sp.dma_start(w2_in[:, c, D + ER:YW], R2[rows, :]).then_inc(w_in, 16)
            sp.wait_ge(consts, 3)
            for k in range(3):
                sp.dma_start(b1_in[k * SB:k * SB + ER, :], B1.rearrange("e r h -> (e r) h")).then_inc(w_in, 16)
                sp.dma_start(b2_in[k * SB:k * SB + ER, :], B2.rearrange("e r h -> (e r) h")).then_inc(w_in, 16)
                sp.dma_start(b1_in[k * SB + ER:k * SB + ER + 1, :], b1.rearrange("(a n) -> a n", a=1)).then_inc(w_in, 16)
                sp.dma_start(b2_in[k * SB + ER:k * SB + ER + 1, :], b2.rearrange("(a n) -> a n", a=1)).then_inc(w_in, 16)
            for w, c0 in ((Wq, 0), (Wk, NH * FD), (Wv, 2 * NH * FD), (Wo, 2 * NH * FD + D)):
                sp.dma_start(aw_in[:, c0:c0 + w.shape[1]], w).then_inc(w_in, 16)
            for i in range(1, 4):
                sp.dma_start(xs[:, i * q:(i + 1) * q, :], xt[:, i * q:(i + 1) * q, :]).then_inc(x_in[i], 16)
            ot = out.rearrange("b l d -> (b l) d").rearrange("(t p) d -> p t d", p=P)
            for i in range(4):
                sp.wait_ge(ff2.done, 2 * (i + 1) * GROUPS // 4)
                sp.dma_start(ot[:, i * q:(i + 1) * q, :], xs[:, i * q:(i + 1) * q, :]).then_inc(stored, 16)
            sp.wait_ge(stored, 64)
        WEIGHT_DMAS = 3 + 3 * HC + 12 + 4

        @block.gpsimd
        def _(pool):
            pool.memset(b1_in[:, :], 0.0).then_inc(consts, 1)
            pool.memset(b2_in[:, :], 0.0).then_inc(consts, 1)
            pool.memset(m.neg_half[:, :], -0.5).then_inc(consts, 1)
            pool.memset(m.ident32[:, :], 0.0).then_inc(consts, 1)
            pool.memset(m.ident16[:, :], 0.0).then_inc(consts, 1)
            pool.memset(row_scale[:, 0:1], 1.0 / (R * WS)).then_inc(consts, 1)
            pool.memset(row_scale[:, 1:2], 1.0 / R).then_inc(consts, 1)
            pool.wait_ge(consts, 7)
            for t in (m.ident32, m.ident16):
                pool.affine_select(out=t[:, :], in_=t[:, :], compare_op=ALU.not_equal, fill=1.0, base=0,
                                   pattern=[[-1, P]], channel_multiplier=1).then_inc(consts, 1)
            n = 9
            for k in range(3):
                for layer in range(2):
                    pool.wait_ge(consts, n)
                    pool.affine_select(out=row_scale[:, layer:layer + 1], in_=row_scale[:, layer:layer + 1],
                                       compare_op=ALU.not_equal, fill=WS ** (layer + 1), base=-(k * SB + ER),
                                       pattern=[[0, 1]], channel_multiplier=1).then_inc(consts, 1)
                    n += 1
            pool.memset(m.ones_tri[:, :], 1.0).then_inc(consts, 1)
            pool.wait_ge(consts, n + 1)
            pool.affine_select(out=m.ones_tri[:, :], in_=m.ones_tri[:, :], compare_op=ALU.is_ge, fill=0.0, base=0,
                               pattern=[[1, LEN]], channel_multiplier=-1).then_inc(consts, 1)
            ff1.gpsimd(pool)
            att.gpsimd(pool)
            ff2.gpsimd(pool)
        CONSTS = 17

        @block.vector
        def _(dve):
            dve.memset(m.zs[:, :, :, :, :], 0.0).then_inc(prep, 1)
            dve.wait_ge(prep, 1)
            dve.memset(m.ve[:, :], 0.0).then_inc(m.started, 1)
            for i in two:
                dve.memset(m.zs[:, :, i, 0:3:2, ER:ER + 1], 1.0).then_inc(prep, 1)
            n = 3
            dve.wait_ge(prep, n)
            dve.wait_ge(consts, CONSTS)
            dve.wait_ge(w_in, 16 * WEIGHT_DMAS)
            for hi, lo, src, scale in ((m.arh, m.arl, ar_in, WS * WS), (m.w1h, m.w1l, w1_in, WS)):
                split(dve, hi[:, :], lo[:, :], src[:, :], scale, prep, n)
                n += 2
            split(dve, m.w2h[:, :, :], m.w2l[:, :, :], w2_in[:, :, :], WS, prep, n)
            n += 2
            for layer, (src, sc, st) in enumerate(((b1_in, b1_sc, m.b1s), (b2_in, b2_sc, m.b2s))):
                dve.tensor_scalar(sc[:, :], src[:, :], row_scale[:, layer:layer + 1], None, ALU.mult).then_inc(prep, 1)
                dve.wait_ge(prep, n + 1)
                dve.tensor_copy(st[:, :], sc[:, :]).then_inc(prep, 1)
                dve.wait_ge(prep, n + 2)
                lo = slice(2 * SB, SK)
                dve.tensor_tensor(st[lo, :], sc[lo, :], st[lo, :], ALU.subtract).then_inc(prep, 1)
                dve.wait_ge(prep, n + 3)
                n += 3
            split(dve, m.wqkh[:, :], m.wqkl[:, :], aw_in[:, 0:2 * NH * FD], WS, prep, n)
            n += 2
            for hi, lo, c0 in ((m.wvh, m.wvl, 2 * NH * FD), (m.woh, m.wol, 2 * NH * FD + D)):
                split(dve, hi[:, :], lo[:, :], aw_in[:, c0:c0 + D], WS, prep, n)
                n += 2
            for v in (m.vf, m.vh, m.vl):
                dve.memset(v[:, :, :, :, :], 0.0).then_inc(prep, 1)
            for which in two:
                dve.memset(m.qk[:, :, which, :, 3, :], 0.0).then_inc(prep, 1)
            n += 5
            dve.wait_ge(prep, n)
            for v in (m.vf, m.vh):
                dve.memset(v[:, :, :, :, HD:HD + 1], WS).then_inc(prep, 1)
            dve.wait_ge(prep, n + 2)
            dve.memset(m.ve[:, :], 0.0).then_inc(ready, 1)

            def x_ready(e, g):
                if isinstance(g, int):
                    e.wait_ge(x_in[g * 4 // GROUPS], 16)
                else:
                    for i in range(4):
                        e.wait_ge(x_in[i], 16)
            ff1.vector(dve, x_ready)
            dve.wait_ge(ff1.done, 2 * GROUPS)
            att.vector(dve)
            dve.wait_ge(att.done, BATCH)
            ff2.vector(dve, lambda e, g: None)

        @block.scalar
        def _(act):
            act.wait_ge(ready, 1)
            ff1.scalar(act)
            att.scalar(act)
            ff2.scalar(act)

        @block.tensor
        def _(pe):
            pe.wait_ge(ready, 1)
            pe.wait_ge(consts, CONSTS)
            ff1.tensor(pe)
            pe.wait_ge(ff1.done, 2 * GROUPS)
            att.tensor(pe)
            pe.wait_ge(att.done, BATCH)
            ff2.tensor(pe)


_INS = ["L0_attn_x", "L0_attn_Wq", "L0_attn_Wk", "L0_attn_Wv", "L0_attn_Wo", "L0_ffn_W1", "L0_ffn_b1", "L0_ffn_A1",
        "L0_ffn_B1", "L0_ffn_R1", "L0_ffn_W2", "L0_ffn_b2", "L0_ffn_A2", "L0_ffn_B2", "L0_ffn_R2"]


def kernel(**inputs):
    import numpy as np
    from concourse import bacc
    from concourse.bass_utils import run_bass_kernel_spmd

    nc = bacc.Bacc("TRN2", target_bir_lowering=False, num_devices=1)
    arrays, args = {}, []
    for name in _INS:
        a = np.ascontiguousarray(inputs[name])
        arrays[f"in_{name}"] = a
        args.append(nc.dram_tensor(f"in_{name}", a.shape, mybir.dt.from_np(a.dtype), kind="ExternalInput").ap())
    args.append(nc.dram_tensor("out_x", (BATCH, LEN, D), F32, kind="ExternalOutput").ap())
    program(nc, *args)
    return run_bass_kernel_spmd(nc, [arrays], core_ids=[0]).results[0]["out_x"]
```

```python
from contextlib import ExitStack

import concourse.bass as bass
from concourse import mybir

F32 = mybir.dt.float32
F16 = mybir.dt.float16
ALU = mybir.AluOpType
ACT = mybir.ActivationFunctionType
AX = mybir.AxisListType

P = 128
BATCH, LEN, D = 32, 256, 128
TILES = BATCH * LEN // P
GT = 4
GN = GT * P
GROUPS = TILES // GT
HID = 512
HC = HID // P
E, R = 3, 8
ER = E * R
YW = D + ER + E
ZW = ER + E
SB = 32
SK = 3 * SB
X_PIECES = (0, 1), (1, 2), (2, 4), (4, 8), (8, 16)
OUT_PIECES = (0, 4), (4, 8), (8, 12), (12, 15), (15, 16)
LN_EPS = 1e-5
WS = 4.0
HIDDEN = (slice(0, 2), slice(0, 2)), (slice(0, 1), slice(2, 3)), (slice(1, 2), slice(3, 4))
GATE_LINKS = 6
FF1 = 3, GROUPS, (GROUPS - 2, -3, GROUPS - 1, -2, GROUPS, -1)
FF1_PE = 3, GROUPS, (GROUPS - 2, -2, GROUPS - 1, GROUPS, -1)
ATT = 3, BATCH, (-3, BATCH - 2, BATCH - 1, -2, BATCH, -1, BATCH + 1)
ATT_ACT = 3, BATCH, (BATCH - 2, -3, BATCH - 1, -2, BATCH, -1, BATCH + 1)
FF2 = 3, GROUPS, (GROUPS,)
ST = LEN // P
NH, FD, HD = 16, 16, 8
SW = LEN + P
ATT_EPS = 1e-12


def split(e, hi, lo, src, scale, hi_made, lo_made):
    e.tensor_scalar(hi, src, scale, None, ALU.mult).then_inc(hi_made, 1)
    e.wait_ge(hi_made, 1)
    e.scalar_tensor_tensor(out=lo, in0=src, scalar=scale, in1=hi, op0=ALU.mult, op1=ALU.subtract).then_inc(lo_made, 1)


def wait_alone(e, semaphore, value, started):
    if not isinstance(value, int):
        value = e.to_reg(value)
    e.wait_ge(started, 1)
    e.wait_ge(semaphore, value)


def exists(g, count):
    return not isinstance(g, int) or 0 <= g < count


def run_parts(e, parts):
    def single(part, g):
        step, before = part[0], part[-1]
        if g in before:
            before[g]()
        step(g, g % 2)

    for g in range(-parts[0][1], 0):
        single(parts[0], g)
    for part, following in zip(parts, [*parts[1:], None]):
        step, lead, count, last, _ = part
        pairs = (count - lead - 2) // 2
        for g in range(2):
            single(part, g)
        with e.Fori(1, 1 + pairs) as pair:
            step(2 * pair, 0)
            step(2 * pair + 1, 1)
        for g in range(2 + 2 * pairs, max(last[:2])):
            single(part, g)
        for g in last:
            single(part if g >= 0 else following, g)


class FeedForward:

    def __init__(self, nc, ctx, name, mem, gates_apart):
        sem = lambda what: ctx.enter_context(nc.semaphore(f"{name}_{what}"))
        self.m = mem
        self.gates_apart = gates_apart
        self.stats = sem("stats")
        self.mean_var = sem("mean_var")
        self.pool_chain = sem("pool_chain")
        self.rstd = sem("rstd")
        self.xn = sem("xn")
        self.xT_ps = sem("xT_ps")
        self.xT_hi = sem("xT_hi")
        self.xT_lo = sem("xT_lo")
        self.z2_ps = sem("z2_ps")
        self.z1_ps = sem("z1_ps")
        self.logits = sem("logits")
        self.exps = sem("exps")
        self.gate_chain = sem("gate_chain")
        self.zs = sem("zs")
        self.zsT_ps = sem("zsT_ps")
        self.zsT2 = sem("zsT2")
        self.zsT1 = sem("zsT1")
        self.h_ps = sem("h_ps")
        self.h_hi = sem("h_hi")
        self.h_lo = sem("h_lo")
        self.y_ps = sem("y_ps")
        self.done = sem("done")

    @staticmethod
    def layers(g):
        return slice(0 if exists(g - 1, GROUPS) else 1, 2 if exists(g + 1, GROUPS) else 1)

    def vector(self, e, x_ready, prepare):
        m = self.m

        def stats(g, p, tiles):
            if tiles[0] == 0:
                x_ready(e, g)
            for t in tiles:
                last = e.bn_stats(m.bn[:, p, t, :], m.x[:, bass.ds(g * GN + t * P, P)])
            if tiles[-1] == GT - 1:
                last.then_inc(self.stats, 1)

        def mean_var(g, p):
            wait_alone(e, self.stats, g + 1, m.started)
            for t in range(GT):
                last = e.bn_aggr(m.mv[:, p, t, :], m.bn[:, p, t, :])
            last.then_inc(self.mean_var, 1)

        def xT_lo(g, p):
            e.wait_ge(self.xT_hi, g + 1)
            e.tensor_tensor(m.xl[:, p, :], m.psT[:, :], m.xh[:, p, :], ALU.subtract).then_inc(self.xT_lo, 1)

        def gates(g, p):
            of = self.layers(g)
            width = of.stop - of.start

            if of.start == 0:
                e.wait_ge(self.z2_ps, g)
            if of.stop == 2:
                e.wait_ge(self.z1_ps, g + 2)
            logits, mx, lg, sm = m.psR[:, :, of, ER:ZW], m.mx[:, :, of], m.lg[:, :, of, :], m.sm[:, :, of]
            ex = m.ex[:, :, of, :]
            e.tensor_reduce(mx, logits, AX.X, ALU.max).then_inc(self.gate_chain, 1)
            e.wait_ge(self.gate_chain, (g + 1) * GATE_LINKS + 1)
            e.tensor_tensor(lg, logits, mx.unsqueeze(3).broadcast_to([P, GT, width, E]),
                            ALU.subtract).then_inc(self.logits, 1)
            if exists(g + 3, GROUPS):
                stats(g + 3, 1 - p, (0, 1))
            e.wait_ge(self.exps, g + 2)
            e.tensor_reduce(sm, ex, AX.X, ALU.add).then_inc(self.gate_chain, 1)
            for i in range(of.start, of.stop):
                last = e.tensor_tensor(m.ze[:, :, i, :].rearrange("p t (e r) -> p t e r", r=R),
                                       m.psR[:, :, i, 0:ER].rearrange("p t (e r) -> p t e r", r=R),
                                       m.ex[:, :, i, :].unsqueeze(3).broadcast_to([P, GT, E, R]), ALU.mult)
            last.then_inc(self.gate_chain, 1)
            e.wait_ge(self.gate_chain, (g + 1) * GATE_LINKS + 2)
            e.reciprocal(sm, sm).then_inc(self.gate_chain, 1)
            e.wait_ge(self.gate_chain, (g + 1) * GATE_LINKS + 4)
            e.tensor_tensor(m.zg[:, :, of, :], m.ze[:, :, of, :], sm.unsqueeze(3).broadcast_to([P, GT, width, ER]),
                            ALU.mult).then_inc(self.gate_chain, 1)
            e.wait_ge(self.gate_chain, (g + 1) * GATE_LINKS + 5)
            e.tensor_copy(m.zs[:, :, of, 0, 0:ER], m.zg[:, :, of, :]).then_inc(self.gate_chain, 1)
            e.tensor_copy(m.zs[:, :, of, 2, 0:ER], m.zg[:, :, of, :])
            e.wait_ge(self.gate_chain, (g + 2) * GATE_LINKS)
            e.tensor_tensor(m.zs[:, :, of, 1, 0:ER], m.zg[:, :, of, :], m.zs[:, :, of, 0, 0:ER],
                            ALU.subtract).then_inc(self.zs, 1)

        def h_lo(g, i):
            e.wait_ge(self.h_hi, 3 * g + i + 1)
            ps, cs = HIDDEN[i]
            e.scalar_tensor_tensor(out=m.hl[:, cs, :], in0=m.psH[cs.start // 2][:, ps, :], scalar=0.0,
                                   in1=m.hh[:, cs, :], op0=ALU.max, op1=ALU.subtract).then_inc(self.h_lo, 1)

        def residual(g):
            for half in range(2):
                e.wait_ge(self.y_ps, 2 * g + half + 1)
                xg = m.x[:, bass.ds(g * GN + half * 2 * P, 2 * P)].rearrange("p (t d) -> p t d", d=D)
                e.scalar_tensor_tensor(out=xg, in0=m.psY[:, half, :, 0:D], scalar=0.5 / (WS * WS), in1=xg,
                                       op0=ALU.mult, op1=ALU.add).then_inc(self.done, 1)

        self.first_gates = lambda: gates(-1, 1)

        def step(g, p):
            if isinstance(g, int) and g == -1 and self.gates_apart:
                pass
            elif exists(g - 1, GROUPS) or exists(g + 1, GROUPS):
                gates(g, p)
            elif exists(g + 3, GROUPS):
                stats(g + 3, 1 - p, (0, 1))
            if exists(g, GROUPS):
                h_lo(g, 0)
            if exists(g + 3, GROUPS):
                stats(g + 3, 1 - p, (2, 3))
            if exists(g - 1, GROUPS):
                residual(g - 1)
            if exists(g + 3, GROUPS):
                mean_var(g + 3, 1 - p)
            if exists(g, GROUPS):
                h_lo(g, 1)
                h_lo(g, 2)
            if isinstance(g, int) and g < 0:
                prepare(g)
            if exists(g + 2, GROUPS):
                xT_lo(g + 2, p)
        return step

    def scalar(self, e):
        m = self.m

        def norm(g, p):
            e.wait_ge(self.rstd, g + 1)
            for t in range(GT):
                last = e.activation(m.xn[:, t, :], m.x[:, bass.ds(g * GN + t * P, P)], ACT.Identity,
                                    bias=m.nm[:, p, t:t + 1], scale=m.rs[:, p, t:t + 1])
            last.then_inc(self.xn, 1)

        def xT_hi(g, p):
            e.wait_ge(self.xT_ps, g + 1)
            e.activation(m.xh[:, p, :], m.psT[:, :], ACT.Copy).then_inc(self.xT_hi, 1)

        def exps(g):
            of = self.layers(g)
            e.wait_ge(self.logits, g + 2)
            e.activation(m.ex[:, :, of, :], m.lg[:, :, of, :], ACT.Exp, scale=WS ** -2).then_inc(self.exps, 1)

        def zsT2(g):
            e.wait_ge(self.zsT_ps, g + 3)
            for half in range(2):
                tok = slice(half * GN // 2, (half + 1) * GN // 2)
                e.activation(m.zsT2[:, tok], m.psZT[0:SK, tok], ACT.Copy).then_inc(self.zsT2, 1)

        def zsT1(g, p):
            e.wait_ge(self.zsT_ps, g + 1)
            e.activation(m.zsT1[:, p, :], m.psZT[0:SK, GN:2 * GN], ACT.Copy).then_inc(self.zsT1, 1)

        def h_hi(g, i):
            e.wait_ge(self.h_ps, 3 * g + i + 1)
            ps, cs = HIDDEN[i]
            e.activation(m.hh[:, cs, :], m.psH[cs.start // 2][:, ps, :], ACT.Relu).then_inc(self.h_hi, 1)

        self.first_exps = lambda: exps(-1)

        def step(g, p):
            if isinstance(g, int) and g == -1 and self.gates_apart:
                pass
            elif exists(g - 1, GROUPS) or exists(g + 1, GROUPS):
                exps(g)
            if exists(g, GROUPS):
                h_hi(g, 0)
                h_hi(g, 1)
            if exists(g - 1, GROUPS):
                zsT2(g - 1)
            if exists(g + 1, GROUPS):
                zsT1(g + 1, 1 - p)
            if exists(g, GROUPS):
                h_hi(g, 2)
            if exists(g + 2, GROUPS):
                xT_hi(g + 2, p)
            if exists(g + 3, GROUPS):
                norm(g + 3, 1 - p)
        return step

    def gpsimd(self, e):
        m = self.m

        def rstd(g, p):
            wait_alone(e, self.mean_var, g + 1, m.started)
            e.tensor_scalar(m.ve[:, 0:GT], m.mv[:, p, :, 1], LN_EPS, None, ALU.add)
            e.tensor_scalar(m.nm[:, p, :], m.mv[:, p, :, 0], -1.0, None, ALU.mult).then_inc(self.pool_chain, 1)
            e.wait_ge(self.pool_chain, 2 * g + 1)
            e.tensor_tensor(m.rs[:, p, :], m.ve[:, 0:GT], m.neg_half[:, 0:GT], ALU.pow).then_inc(self.pool_chain, 1)
            e.wait_ge(self.pool_chain, 2 * g + 2)
            e.tensor_tensor(m.nm[:, p, :], m.nm[:, p, :], m.rs[:, p, :], ALU.mult).then_inc(self.rstd, 1)

        def step(g, p):
            if exists(g + 3, GROUPS):
                rstd(g + 3, 1 - p)
        return step

    def tensor(self, e):
        m = self.m

        def mm(out, lhsT, rhs, start, stop):
            return e.matmul(out, lhsT, rhs, start=start, stop=stop, skip_group_check=True)

        def xT(g):
            e.wait_ge(self.xn, g + 1)
            if not (isinstance(g, int) and g == 0):
                e.wait_ge(self.xT_lo, g)
            for t in range(GT):
                last = e.transpose(m.psT[:, t * P:(t + 1) * P], m.xn[:, t, :], m.ident32[:, :])
            last.then_inc(self.xT_ps, 1)

        def z1(g, p, opens):
            if opens and g > 0:
                e.wait_ge(self.zs, g)
            if isinstance(g, int) and g == 0:
                e.wait_ge(m.weights, 1)
            for t in range(GT):
                out, tok = m.psR[:, t, 1, 0:ZW], slice(t * P, (t + 1) * P)
                e.wait_ge(self.xT_hi, g + 1)
                mm(out, m.xh[:, p, tok], m.arh[:, :], opens and t % 2 == 0, False)
                mm(out, m.xh[:, p, tok], m.arl[:, :], False, False)
                e.wait_ge(self.xT_lo, g + 1)
                last = mm(out, m.xl[:, p, tok], m.arh[:, :], False, True)
            last.then_inc(self.z1_ps, 1)

        def zsT(g):
            of = self.layers(g)
            e.wait_ge(self.zs, g + 2)
            for i in range(of.start, of.stop):
                for t in range(GT):
                    last = e.transpose(m.psZT[0:SK, i * GN + t * P:i * GN + (t + 1) * P],
                                       m.zs[:, t, i, :, :].rearrange("p k c -> p (k c)"), m.ident16[:, :])
            last.then_inc(self.zsT_ps, 1)

        def hidden(g, p, i):
            if not (isinstance(g, int) and g == 0):
                e.wait_ge(self.h_lo, 3 * (g - 1) + i + 1)
            if i == 0:
                e.wait_ge(self.zsT1, g + 1)
                if isinstance(g, int) and g == 0:
                    e.wait_ge(m.weights, 3)
            for c in range(HIDDEN[i][1].start, HIDDEN[i][1].stop):
                cols, out = slice(c * P, (c + 1) * P), m.psH[c // 2][:, c % 2, :]
                mm(out, m.w1h[:, cols], m.xh[:, p, :], True, False)
                mm(out, m.w1l[:, cols], m.xh[:, p, :], False, False)
                mm(out, m.w1h[:, cols], m.xl[:, p, :], False, False)
                last = mm(out, m.b1s[:, cols], m.zsT1[:, p, :], False, True)
            last.then_inc(self.h_ps, 1)

        def second(g, i):
            e.wait_ge(self.h_lo, 3 * g + i + 1)
            if isinstance(g, int) and g == 0:
                e.wait_ge(m.weights, 5)
            for half in range(2):
                if i == 0 and not (isinstance(g, int) and g == 0):
                    e.wait_ge(self.done, 2 * g - 1 + half)
                for c in range(HIDDEN[i][1].start, HIDDEN[i][1].stop):
                    for t in (2 * half, 2 * half + 1):
                        out, tok = m.psY[:, half, t % 2, 0:YW], slice(t * P, (t + 1) * P)
                        mm(out, m.hh[:, c, tok], m.w2h[:, c, :], c == 0 and t % 2 == 0, False)
                        mm(out, m.hh[:, c, tok], m.w2l[:, c, :], False, False)
                        last = mm(out, m.hl[:, c, tok], m.w2h[:, c, :], False, c == HC - 1)
            if i == 2:
                last.then_inc(self.z2_ps, 1)

        def adapters2(g):
            for half in range(2):
                e.wait_ge(self.zsT2, 2 * g + half + 1)
                for t in (2 * half, 2 * half + 1):
                    last = mm(m.psY[:, half, t % 2, 0:D], m.zsT2[:, t * P:(t + 1) * P], m.b2s[:, :], False, True)
                last.then_inc(self.y_ps, 1)

        def step(g, p):
            if exists(g, GROUPS):
                hidden(g, p, 0)
                hidden(g, p, 1)
            if exists(g - 1, GROUPS) or exists(g + 1, GROUPS):
                zsT(g)
            if exists(g, GROUPS):
                hidden(g, p, 2)
            if exists(g - 1, GROUPS):
                adapters2(g - 1)
            if exists(g + 2, GROUPS):
                xT(g + 2)
            if exists(g, GROUPS):
                second(g, 0)
                second(g, 1)
                second(g, 2)
            if exists(g + 2, GROUPS):
                z1(g + 2, p, opens=not exists(g, GROUPS))
        return step


class Attention:

    def __init__(self, nc, ctx, name, mem):
        sem = lambda what: ctx.enter_context(nc.semaphore(f"{name}_{what}"))
        self.m = mem
        self.stats = sem("stats")
        self.mean_var = sem("mean_var")
        self.pool_chain = sem("pool_chain")
        self.rstd = sem("rstd")
        self.xn = sem("xn")
        self.xT_ps = sem("xT_ps")
        self.xT_hi = sem("xT_hi")
        self.xT_lo = sem("xT_lo")
        self.qk_ps = sem("qk_ps")
        self.qk_hi = sem("qk_hi")
        self.qk_lo = sem("qk_lo")
        self.hi_again = sem("hi_again")
        self.stack_ps = sem("stack_ps")
        self.stacks = sem("stacks")
        self.v_ps = sem("v_ps")
        self.v_hi = sem("v_hi")
        self.v_lo = sem("v_lo")
        self.s_ps = sem("s_ps")
        self.squares = sem("squares")
        self.masked = sem("masked")
        self.sums_ps = sem("sums_ps")
        self.sums = sem("sums")
        self.ytok_ps = sem("ytok_ps")
        self.y_chain = sem("y_chain")
        self.y = sem("y")
        self.yT_ps = sem("yT_ps")
        self.yT_hi = sem("yT_hi")
        self.yT_lo = sem("yT_lo")
        self.out_ps = sem("out_ps")
        self.done = sem("done")

    def vector(self, e):
        m = self.m

        def tile(b, t):
            return m.x[:, bass.ds(b * LEN + t * P, P)]

        def stats(b):
            for t in range(ST):
                last = e.bn_stats(m.bn[:, 0, t, :], tile(b, t))
            last.then_inc(self.stats, 1)

        def mean_var(b):
            wait_alone(e, self.stats, b + 1, m.started)
            for t in range(ST):
                last = e.bn_aggr(m.mv[:, 0, t, :], m.bn[:, 0, t, :])
            last.then_inc(self.mean_var, 1)

        def norm(b):
            e.wait_ge(self.rstd, b + 1)
            if not (isinstance(b, int) and b == 0):
                e.wait_ge(self.xT_ps, b)
            for t in range(ST):
                last = e.tensor_scalar(m.xn[:, t, :], tile(b, t), m.mv[:, 0, t, 0:1], m.rs[:, 0, t:t + 1],
                                       ALU.subtract, ALU.mult)
            last.then_inc(self.xn, 1)

        def xT_lo(b, p):
            e.wait_ge(self.xT_hi, b + 1)
            e.tensor_tensor(m.axl[:, p, :], m.psT[:, 0:LEN], m.axh[:, p, :], ALU.subtract).then_inc(self.xT_lo, 1)

        def qk_lo(b, which):
            e.wait_ge(self.qk_hi, 2 * b + 2)
            e.tensor_tensor(m.qk[:, :, which, :, 1 + which, :], m.psQK[:, :, which, :, :],
                            m.qk[:, :, which, :, 0, :], ALU.subtract).then_inc(self.qk_lo, 1)

        def hi_again(b, which):
            e.wait_ge(self.qk_hi, 2 * b + 2)
            e.tensor_copy(m.qk[:, :, which, :, 2 - which, :], m.qk[:, :, which, :, 0, :]).then_inc(self.hi_again, 1)

        def stack(b, p, which, half):
            e.wait_ge(self.stack_ps, 4 * b + 2 * which + half + 1)
            us = slice(4 * half, 4 * half + 4)
            e.tensor_copy(m.stack[which][:, p, us, :], m.psSt[:, us, :]).then_inc(self.stacks, 1)

        def v_lo(b, p):
            e.wait_ge(self.v_hi, b + 1)
            e.tensor_tensor(m.vl[:, p, :, :, 0:HD], m.psV, m.vh[:, p, :, :, 0:HD], ALU.subtract).then_inc(self.v_lo, 1)

        def normalise(b):
            n = b * 2
            e.wait_ge(self.ytok_ps, b + 1)
            e.tensor_scalar(m.den[:, :, :], m.psYt[:, :, :, HD], 2 * WS * ATT_EPS, None, ALU.add).then_inc(self.y_chain, 1)
            e.wait_ge(self.y_chain, n + 1)
            e.reciprocal(m.den[:, :, :], m.den[:, :, :]).then_inc(self.y_chain, 1)
            e.wait_ge(self.y_chain, n + 2)
            e.tensor_tensor(m.yn[:, :, :, :], m.psYt[:, :, :, 0:HD],
                            m.den[:, :, :].unsqueeze(3).broadcast_to([P, ST, NH, HD]), ALU.mult).then_inc(self.y, 1)

        def yT_lo(b):
            e.wait_ge(self.yT_hi, b + 1)
            e.tensor_tensor(m.yl[:, :], m.psT[:, 0:LEN], m.yh[:, :], ALU.subtract).then_inc(self.yT_lo, 1)

        def residual(b):
            e.wait_ge(self.out_ps, b + 1)
            xb = m.x[:, bass.ds(b * LEN, LEN)]
            e.scalar_tensor_tensor(out=xb, in0=m.psT[:, LEN:2 * LEN], scalar=1.0 / WS, in1=xb, op0=ALU.mult,
                                   op1=ALU.add).then_inc(self.done, 1)

        def step(b, p):
            prev, nxt, nxt2, nxt3 = (exists(b + k, BATCH) for k in (-1, 1, 2, 3))
            if exists(b - 2, BATCH):
                residual(b - 2)
            if nxt:
                qk_lo(b + 1, 0)
                qk_lo(b + 1, 1)
                hi_again(b + 1, 0)
                hi_again(b + 1, 1)
            if nxt3:
                stats(b + 3)
            if nxt2:
                xT_lo(b + 2, p)
            if nxt3:
                mean_var(b + 3)
            if prev:
                normalise(b - 1)
            if nxt:
                v_lo(b + 1, 1 - p)
                stack(b + 1, 1 - p, 0, 0)
                stack(b + 1, 1 - p, 0, 1)
            if prev:
                yT_lo(b - 1)
            if nxt:
                stack(b + 1, 1 - p, 1, 0)
            if nxt3:
                norm(b + 3)
            if nxt:
                stack(b + 1, 1 - p, 1, 1)
        return step

    def scalar(self, e):
        m = self.m

        def square(b, k, first):
            e.wait_ge(self.s_ps, 8 * b + k + 1)
            if not first:
                e.wait_ge(self.sums_ps, 4 * (b - 1) + k // 2 + 1)
            e.activation(m.G[:, k, :, :], m.psS[k % 2][:, :, 0:SW], ACT.Square, bias=1.0,
                         scale=0.25 / (WS * WS)).then_inc(self.squares, 1)

        def sums(b, half):
            e.wait_ge(self.sums_ps, 4 * b + 2 * half + 2)
            e.activation(m.YT[:, half, :], m.psU[:, half, :], ACT.Copy).then_inc(self.sums, 1)

        def xT_hi(b, p):
            e.wait_ge(self.xT_ps, b + 1)
            e.activation(m.axh[:, p, :], m.psT[:, 0:LEN], ACT.Copy).then_inc(self.xT_hi, 1)

        def v_hi(b, p):
            e.wait_ge(self.v_ps, b + 1)
            for t in range(ST):
                e.activation(m.vf[:, p, t, :, :, 0:HD], m.psV[:, t, :, :].rearrange("p (u r) c -> p u r c", r=2),
                             ACT.Copy)
            e.activation(m.vh[:, p, :, :, 0:HD], m.psV, ACT.Copy).then_inc(self.v_hi, 1)

        def qk_hi(b, t):
            e.wait_ge(self.qk_ps, 2 * b + t + 1)
            e.activation(m.qk[:, t, :, :, 0, :], m.psQK[:, t, :, :, :], ACT.Copy).then_inc(self.qk_hi, 1)

        def yT_hi(b):
            e.wait_ge(self.yT_ps, b + 1)
            e.activation(m.yh[:, :], m.psT[:, 0:LEN], ACT.Copy).then_inc(self.yT_hi, 1)

        def step(b, p):
            prev, main, nxt, nxt2 = (exists(b + k, BATCH) for k in (-1, 0, 1, 2))
            zero = isinstance(b, int) and b == 0
            if nxt:
                qk_hi(b + 1, 0)
                qk_hi(b + 1, 1)
            if main:
                square(b, 0, zero)
                square(b, 1, zero)
            if prev:
                sums(b - 1, 1)
            if nxt2:
                xT_hi(b + 2, p)
            if main:
                square(b, 2, zero)
                square(b, 3, zero)
            if nxt:
                v_hi(b + 1, 1 - p)
            if main:
                square(b, 4, zero)
                square(b, 5, zero)
                sums(b, 0)
            if prev:
                yT_hi(b - 1)
            if main:
                square(b, 6, zero)
                square(b, 7, zero)
        return step

    def gpsimd(self, e):
        m = self.m

        def rstd(b):
            wait_alone(e, self.mean_var, b + 1, m.started)
            e.tensor_scalar(m.ve[:, 0:ST], m.mv[:, 0, 0:ST, 1], LN_EPS, None, ALU.add).then_inc(self.pool_chain, 1)
            e.wait_ge(self.pool_chain, b + 1)
            e.tensor_tensor(m.rs[:, 0, 0:ST], m.ve[:, 0:ST], m.neg_half[:, 0:ST], ALU.pow).then_inc(self.rstd, 1)

        def mask(b, k):
            wait_alone(e, self.squares, 8 * b + k + 1, m.started)
            for h in range(2):
                g = m.G[:, k, h, :].rearrange("p (c n) -> p c n", n=P)[:, 0:3:2, :]
                last = e.affine_select(out=g, in_=g, compare_op=ALU.is_ge, fill=0.0, base=0,
                                       pattern=[[0, 2], [1, P]], channel_multiplier=-1)
            last.then_inc(self.masked, 1)

        def step(b, p):
            main = exists(b, BATCH)
            if main:
                for k in range(4):
                    mask(b, k)
            if exists(b + 3, BATCH):
                rstd(b + 3)
            if main:
                for k in range(4, NH // 2):
                    mask(b, k)
        return step

    def tensor(self, e):
        m = self.m

        def mm(out, lhsT, rhs, start, stop, **kw):
            return e.matmul(out, lhsT, rhs, start=start, stop=stop, skip_group_check=True, **kw)


        def xT(b, free):
            e.wait_ge(self.xn, b + 1)
            if free:
                e.wait_ge(self.done, b - 3)
            for t in range(ST):
                last = e.transpose(m.psT[:, t * P:(t + 1) * P], m.xn[:, t, :], m.ident32[:, :])
            last.then_inc(self.xT_ps, 1)

        def v(b, p, tokens, free):
            e.wait_ge(self.xT_lo, b + 2 if tokens else b + 1)
            if free:
                e.wait_ge(self.done, b - 2)
            for t in range(ST):
                out, tok = m.psT[:, LEN + t * P:LEN + (t + 1) * P], slice(t * P, (t + 1) * P)
                mm(out, m.axh[:, p, tok], m.wvh[:, :], t == 0, False)
                mm(out, m.axh[:, p, tok], m.wvl[:, :], False, False)
                last = mm(out, m.axl[:, p, tok], m.wvh[:, :], False, True)
            last.then_inc(self.v_ps, 1)

        def project(b, p, t, stacks):
            e.wait_ge(self.xT_lo, b + 1)
            if stacks:
                e.wait_ge(self.stacks, 4 * (b - 1) + t + 3)
            out, tok = m.psH[0][:, t, :], slice(t * P, (t + 1) * P)
            mm(out, m.axh[:, p, tok], m.wqkh[:, :], True, False)
            mm(out, m.axh[:, p, tok], m.wqkl[:, :], False, False)
            mm(out, m.axl[:, p, tok], m.wqkh[:, :], False, True).then_inc(self.qk_ps, 1)

        def stack(b, which, half):
            if which == 0:
                e.wait_ge(self.qk_lo, 2 * b + 2)
                e.wait_ge(self.hi_again, 2 * b + 2)
            else:
                e.wait_ge(self.stacks, 4 * b + half + 1)
            for u in range(4 * half, 4 * half + 4):
                for t in range(ST):
                    rows = m.qk[:, t, which, 2 * u:2 * u + 2, :, :].rearrange("p h k c -> p (h k c)")
                    last = e.transpose(m.psSt[:, u, t * P:(t + 1) * P], rows, m.ident16[:, :])
            last.then_inc(self.stack_ps, 1)

        def scores(b, p, k, first):
            if k >= 2 or not first:
                e.wait_ge(self.squares, 8 * b + k - 1)
            if k % 4 == 0:
                e.wait_ge(self.stacks, 4 * b + 3 + k // 4)
            for h in range(2):
                rows = slice(64 * h, 64 * h + 64)
                for kt, (n0, c0) in enumerate(((0, 0), (P, LEN))):
                    last = mm(m.psS[k % 2][:, h, c0:c0 + LEN - n0], m.stack[1][rows, p, k, kt * P:(kt + 1) * P],
                              m.stack[0][rows, p, k, n0:LEN], kt == 0, kt == 1, tile_position=(64 * h, 0))
            last.then_inc(self.s_ps, 1)

        def head_sums(b, p, j, free):
            e.wait_ge(self.masked, 8 * b + 2 * j + 2)
            if j == 0:
                e.wait_ge(self.v_lo, b + 1)
                if free:
                    e.wait_ge(self.sums, 2 * b)
            if j == 2:
                e.wait_ge(self.sums, 2 * b + 1)
            out = m.psU[:, j // 2, :]
            for kt, n0, c0 in ((0, 0, 0), (1, P, LEN)):
                for i in range(4):
                    v = m.vf[:, p, kt, 4 * (j // 2) + i, :, :].rearrange("p r c -> p (r c)")
                    last = mm(out[32 * i:32 * i + 32, n0:LEN], v[:, 32 * (j % 2):32 * (j % 2) + 32],
                              m.G[:, 2 * j + i // 2, i % 2, c0:c0 + LEN - n0], kt == 0 and j % 2 == 0,
                              kt == 1 and j % 2 == 1, tile_position=(0, 32 * i))
            last.then_inc(self.sums_ps, 1)

        def ytok(b, p, projected, stacked):
            e.wait_ge(self.sums, 2 * b + 2)
            if projected:
                e.wait_ge(self.qk_lo, 2 * b + 6)
            elif stacked:
                e.wait_ge(self.stacks, 4 * b + 8)
            for t in range(ST):
                for j in range(2):
                    mm(m.psYf[:, t, j, :], m.YT[:, j, t * P:(t + 1) * P], m.ident32[:, :], j == 0, False,
                       is_transpose=True)
                for kt in range(t + 1):
                    upto = m.ones_tri[:, (t - kt) * P:(t - kt + 1) * P]
                    for vv in (m.vh, m.vl):
                        last = mm(m.psYt[:, t, :, 0:HD + 1], upto, vv[:, p, kt, :, :], False, kt == t)
            last.then_inc(self.ytok_ps, 1)

        def yT(b, v_there):
            e.wait_ge(self.y, b + 1)
            if v_there:
                e.wait_ge(self.v_lo, b + 3)
            else:
                e.wait_ge(self.done, b)
            for t in range(ST):
                last = e.transpose(m.psT[:, t * P:(t + 1) * P], m.yn[:, t, :, :].rearrange("p h c -> p (h c)"),
                                   m.ident32[:, :])
            last.then_inc(self.yT_ps, 1)

        def output(b):
            e.wait_ge(self.yT_lo, b + 1)
            for t in range(ST):
                out, tok = m.psT[:, LEN + t * P:LEN + (t + 1) * P], slice(t * P, (t + 1) * P)
                mm(out, m.yh[:, tok], m.woh[:, :], t == 0, False)
                mm(out, m.yh[:, tok], m.wol[:, :], False, False)
                last = mm(out, m.yl[:, tok], m.woh[:, :], False, True)
            last.then_inc(self.out_ps, 1)

        def begin():
            project(0, 0, 0, False)
            project(0, 0, 1, False)
            xT(1, False)

        def step(b, p):
            prev, main, nxt, nxt2 = (exists(b + k, BATCH) for k in (-1, 0, 1, 2))
            zero, begun = (isinstance(b, int) and b == k for k in (0, -1))
            if zero:
                scores(b, p, 0, zero)
                scores(b, p, 1, zero)
            if nxt and not begun:
                project(b + 1, 1 - p, 0, main)
                project(b + 1, 1 - p, 1, main)
            if exists(b - 2, BATCH):
                output(b - 2)
            if main and not zero:
                scores(b, p, 0, zero)
                scores(b, p, 1, zero)
            if prev:
                head_sums(b - 1, 1 - p, 3, True)
            if main:
                scores(b, p, 2, zero)
            if nxt2 and not begun:
                xT(b + 2, not (isinstance(b, int) and b < 2))
            if main:
                scores(b, p, 3, zero)
            if prev:
                ytok(b - 1, 1 - p, nxt, main)
            if main:
                head_sums(b, p, 0, not zero)
            if nxt:
                v(b + 1, 1 - p, nxt2, not (isinstance(b, int) and b < 2))
            if main:
                scores(b, p, 4, zero)
            if nxt:
                if prev:
                    e.wait_ge(self.y, b)
                stack(b + 1, 0, 0)
                stack(b + 1, 0, 1)
            if main:
                scores(b, p, 5, zero)
                head_sums(b, p, 1, not zero)
            if prev:
                yT(b - 1, nxt)
            if nxt:
                stack(b + 1, 1, 0)
                stack(b + 1, 1, 1)
            if main:
                scores(b, p, 6, zero)
                scores(b, p, 7, zero)
                head_sums(b, p, 2, not zero)
        return step, begin


class Memory:
    pass


def program(nc, x, Wq, Wk, Wv, Wo, W1, b1, A1, B1, R1, W2, b2, A2, B2, R2, out):
    with ExitStack() as ctx:
        m = Memory()

        def sb(name, shape, dt):
            return ctx.enter_context(nc.sbuf_tensor(name, shape, dt))

        def ps(name, shape, dt=F32):
            return ctx.enter_context(nc.psum_tensor(name, shape, dt))

        def sem(name):
            return ctx.enter_context(nc.semaphore(name))

        m.x = sb("x_sb", [P, TILES * D], F32)
        w1_in = sb("w1_in", [P, HID], F32)
        ar_in = sb("ar_in", [P, ZW], F32)
        w2_in = sb("w2_in", [P, HC, YW], F32)
        b1_in = sb("b1_in", [SK, HID], F32)
        b2_in = sb("b2_in", [SK, D], F32)
        row_scale = sb("row_scale", [SK, 2], F32)
        b1_sc = sb("b1_sc", [SK, HID], F32)
        b2_sc = sb("b2_sc", [SK, D], F32)
        m.w1h, m.w1l = sb("w1h", [P, HID], F16), sb("w1l", [P, HID], F16)
        m.arh, m.arl = sb("arh", [P, ZW], F16), sb("arl", [P, ZW], F16)
        m.w2h, m.w2l = sb("w2h", [P, HC, YW], F16), sb("w2l", [P, HC, YW], F16)
        m.b1s, m.b2s = sb("b1s", [SK, HID], F16), sb("b2s", [SK, D], F16)
        m.ident32, m.ident16 = sb("ident32", [P, P], F32), sb("ident16", [P, P], F16)
        m.neg_half = sb("neg_half", [P, GT], F32)
        m.bn = sb("bn", [P, 2, GT, 6], F32)
        m.mv = sb("mv", [P, 2, GT, 2], F32)
        m.ve = sb("ve", [P, GT], F32)
        m.rs = sb("rs", [P, 2, GT], F32)
        m.nm = sb("nm", [P, 2, GT], F32)
        m.xn = sb("xn", [P, GT, D], F32)
        m.xh, m.xl = sb("xh", [P, 2, GN], F16), sb("xl", [P, 2, GN], F16)
        two = range(2)
        m.mx = sb("mx", [P, GT, 2], F32)
        m.lg = sb("lg", [P, GT, 2, E], F32)
        m.ex = sb("ex", [P, GT, 2, E], F32)
        m.sm = sb("sm", [P, GT, 2], F32)
        m.ze = sb("ze", [P, GT, 2, ER], F32)
        m.zg = sb("zg", [P, GT, 2, ER], F32)
        m.zs = sb("zs", [P, GT, 2, 3, SB], F16)
        m.zsT2 = sb("zsT2", [SK, GN], F16)
        m.zsT1 = sb("zsT1", [SK, 2, GN], F16)
        m.hh, m.hl = sb("hh", [P, HC, GN], F16), sb("hl", [P, HC, GN], F16)

        aw_in = sb("aw_in", [P, 2 * NH * FD + 2 * D], F32)
        aw_sc = sb("aw_sc", aw_in.shape, F32)
        m.awh, m.awl = sb("awh", aw_in.shape, F16), sb("awl", aw_in.shape, F16)
        (m.wqkh, m.wvh, m.woh), (m.wqkl, m.wvl, m.wol) = (
            [w[:, c0:c1] for c0, c1 in ((0, 2 * NH * FD), (2 * NH * FD, 2 * NH * FD + D),
                                        (2 * NH * FD + D, 2 * NH * FD + 2 * D))] for w in (m.awh, m.awl))
        m.ones_tri = sb("ones_tri", [P, LEN], F16)
        m.axh, m.axl = sb("axh", [P, 2, LEN], F16), sb("axl", [P, 2, LEN], F16)
        m.qk = sb("qk", [P, ST, 2, NH, 4, FD], F16)
        m.stack = [sb(n, [P, 2, NH // 2, LEN], F16) for n in ("q_stack", "k_stack")]
        m.vf = sb("vf", [P, 2, ST, NH // 2, 2, 3 * 16], F32)
        m.vh, m.vl = sb("vh", [P, 2, ST, NH, HD + 1], F16), sb("vl", [P, 2, ST, NH, HD + 1], F16)
        m.G = sb("G", [P, NH // 2, 2, SW], F32)
        m.YT = sb("YT", [P, 2, LEN], F32)
        m.den = sb("den", [P, ST, NH], F32)
        m.yn = sb("yn", [P, ST, NH, HD], F32)
        m.yh, m.yl = sb("yh", [P, LEN], F16), sb("yl", [P, LEN], F16)

        m.psH = [ps(f"psH{i}", [P, 2, GN]) for i in two]
        m.psY = ps("psY", [P, 2, 2, 2 * P])
        m.psT = ps("psT", [P, GN])
        bank = ps("psB", [P, GN])
        m.psR = m.psY[:, :, :, :].rearrange("p a b n -> p (a b) n")[:, :, D:D + 2 * SB].rearrange(
            "p t (i c) -> p t i c", c=SB)
        m.psZT = bank[:, :].bitcast(F16)
        m.psQK = m.psH[0][:, :, :].rearrange("p t (w h c) -> p t w h c", w=2, c=FD)
        m.psSt = m.psH[0][:, :, :].rearrange("p a n -> p (a n)").bitcast(F16).rearrange("p (u n) -> p u n", n=LEN)
        m.psYf = m.psH[0][:, :, 0:2 * P].rearrange("p t (j c) -> p t j c", c=P)
        m.psYt = m.psH[0][:, :, 0:2 * P].rearrange("p t (h c) -> p t h c", c=16)
        m.psS = [m.psH[1][:, :, :], m.psY[:, :, :, :].rearrange("p a b n -> p a (b n)")]
        m.psV = m.psT[:, LEN:2 * LEN].rearrange("p (t h c) -> p t h c", h=NH, c=HD)
        m.psU = bank[:, :].rearrange("p (j n) -> p j n", n=LEN)

        x_in = [sem(f"x_in{i}") for i in range(len(X_PIECES))]
        routing_in, first_in, second_in, att_in = (sem(f"{n}_in") for n in ("routing", "first", "second", "att"))
        consts = sem("consts")
        ident16 = sem("ident16_made")
        pads = sem("pads")
        m.started = sem("started")
        hi_made = [sem(f"hi_made{i}") for i in range(3)]
        stack_chain = [sem(f"stack_chain{i}") for i in range(2)]
        m.weights = sem("weights")
        att_prep = sem("att_prep")
        stored = sem("stored")
        ff1 = FeedForward(nc, ctx, "ff1", m, gates_apart=False)
        att = Attention(nc, ctx, "att", m)
        ff2 = FeedForward(nc, ctx, "ff2", m, gates_apart=True)

        block = ctx.enter_context(nc.Block())

        @block.sync
        def _(sp):
            xt = x.rearrange("b l d -> (b l) d").rearrange("(t p) d -> p t d", p=P)
            xs = m.x[:, :].rearrange("p (t d) -> p t d", d=D)

            def load_x(i):
                tiles = slice(GT * X_PIECES[i][0], GT * X_PIECES[i][1])
                sp.dma_start(xs[:, tiles, :], xt[:, tiles, :]).then_inc(x_in[i], 16)

            load_x(0)
            sp.dma_start(ar_in[:, 0:ER].rearrange("p (e r) -> p e r", r=R), A1.rearrange("e d r -> d e r")).then_inc(routing_in, 16)
            sp.dma_start(ar_in[:, ER:ZW], R1).then_inc(routing_in, 16)
            load_x(1)
            sp.dma_start(w1_in[:, :], W1).then_inc(first_in, 16)
            sp.wait_ge(consts, 3)
            for k in range(3):
                sp.dma_start(b1_in[k * SB:k * SB + ER, :], B1.rearrange("e r h -> (e r) h")).then_inc(first_in, 16)
                sp.dma_start(b1_in[k * SB + ER:k * SB + ER + 1, :], b1.rearrange("(a n) -> a n", a=1)).then_inc(first_in, 16)
            load_x(2)
            sp.dma_start(w2_in[:, :, 0:D], W2.rearrange("(c p) d -> p c d", p=P)).then_inc(second_in, 16)
            for c in range(HC):
                rows = slice(c * P, (c + 1) * P)
                sp.dma_start(w2_in[:, c, D:D + ER].rearrange("p (e r) -> p e r", r=R),
                             A2[:, rows, :].rearrange("e d r -> d e r")).then_inc(second_in, 16)
            sp.dma_start(w2_in[:, :, D + ER:YW], R2.rearrange("(c p) e -> p c e", p=P)).then_inc(second_in, 16)
            for k in range(3):
                sp.dma_start(b2_in[k * SB:k * SB + ER, :], B2.rearrange("e r h -> (e r) h")).then_inc(second_in, 16)
                sp.dma_start(b2_in[k * SB + ER:k * SB + ER + 1, :], b2.rearrange("(a n) -> a n", a=1)).then_inc(second_in, 16)
            for i in range(3, len(X_PIECES)):
                load_x(i)
            for w, c0 in ((Wq, 0), (Wk, NH * FD)):
                for j in range(NH // 8):
                    cols = slice(j * 8 * FD, (j + 1) * 8 * FD)
                    for r in range(2):
                        sp.dma_start(aw_in[:, c0 + cols.start:c0 + cols.stop].rearrange(
                            "p (r i c) -> p r i c", r=2, c=FD)[:, r, :, :],
                            w[:, cols].rearrange("p (i r c) -> p i r c", r=2, c=FD)[:, :, r, :]).then_inc(att_in, 16)
            for w, c0 in ((Wv, 2 * NH * FD), (Wo, 2 * NH * FD + D)):
                sp.dma_start(aw_in[:, c0:c0 + w.shape[1]], w).then_inc(att_in, 16)
            ot = out.rearrange("b l d -> (b l) d").rearrange("(t p) d -> p t d", p=P)
            for g0, g1 in OUT_PIECES:
                tiles = slice(GT * g0, GT * g1)
                sp.wait_ge(ff2.done, 2 * g1)
                sp.dma_start(ot[:, tiles, :], xs[:, tiles, :]).then_inc(stored, 16)
            sp.wait_ge(stored, 16 * len(OUT_PIECES))
        ROUTING_DMAS, FIRST_DMAS, SECOND_DMAS, ATT_DMAS = 2, 1 + 6, 2 + HC + 6, 2 * NH // 4 + 2

        @block.gpsimd
        def _(pool):
            pool.memset(b1_in[:, :], 0.0).then_inc(consts, 1)
            pool.memset(b2_in[:, :], 0.0).then_inc(consts, 1)
            pool.memset(m.neg_half[:, :], -0.5).then_inc(consts, 1)
            pool.memset(m.ident32[:, :], 0.0).then_inc(consts, 1)
            pool.memset(row_scale[:, 0:1], 1.0 / (R * WS)).then_inc(consts, 1)
            pool.memset(row_scale[:, 1:2], 1.0 / R).then_inc(consts, 1)
            pool.wait_ge(consts, 6)
            pool.affine_select(out=m.ident32[:, :], in_=m.ident32[:, :], compare_op=ALU.not_equal, fill=1.0, base=0,
                               pattern=[[-1, P]], channel_multiplier=1).then_inc(consts, 1)
            n = 7
            for k in range(3):
                for layer in range(2):
                    pool.wait_ge(consts, n)
                    pool.affine_select(out=row_scale[:, layer:layer + 1], in_=row_scale[:, layer:layer + 1],
                                       compare_op=ALU.not_equal, fill=WS ** (layer + 1), base=-(k * SB + ER),
                                       pattern=[[0, 1]], channel_multiplier=1).then_inc(consts, 1)
                    n += 1

            def attention_masks():
                pool.memset(m.ones_tri[:, :], 1.0).then_inc(att_prep, 1)
                for which in two:
                    pool.memset(m.qk[:, :, which, :, 3, :], 0.0).then_inc(att_prep, 1)
                pool.wait_ge(att_prep, 3)
                pool.affine_select(out=m.ones_tri[:, :], in_=m.ones_tri[:, :], compare_op=ALU.is_ge, fill=0.0, base=0,
                                   pattern=[[1, LEN]], channel_multiplier=-1).then_inc(att_prep, 1)

            def attention_pads():
                pool.memset(m.vf[:, :, :, :, :, :], 0.0).then_inc(att_prep, 1)
                pool.wait_ge(att_prep, 5)
                for t in range(ST):
                    pool.memset(m.vf[:, :, t, :, :, HD:HD + 1], WS).then_inc(att_prep, 1)
                pool.memset(m.vh[:, :, :, :, HD:HD + 1], WS).then_inc(att_prep, 1)
                pool.memset(m.vl[:, :, :, :, HD:HD + 1], 0.0).then_inc(att_prep, 1)

            def attention_weights_hi():
                pool.wait_ge(att_in, 16 * ATT_DMAS)
                pool.tensor_scalar(aw_sc[:, :], aw_in[:, :], WS, None, ALU.mult).then_inc(att_prep, 1)
                pool.tensor_scalar(m.awh[:, :], aw_in[:, :], WS, None, ALU.mult).then_inc(att_prep, 1)

            def attention_weights_lo():
                pool.wait_ge(att_prep, 11)
                pool.tensor_tensor(m.awl[:, :], aw_sc[:, :], m.awh[:, :], ALU.subtract).then_inc(att_prep, 1)

            run_parts(pool, [(ff1.gpsimd(pool), *FF1, {0: attention_masks, 1: attention_pads, 12: attention_weights_hi,
                                                       13: attention_weights_lo}),
                             (att.gpsimd(pool), *ATT, {}),
                             (ff2.gpsimd(pool), *FF2, {})])
        CONSTS, ATT_PREP = 13, 12

        @block.vector
        def _(dve):
            dve.memset(m.zs[:, :, :, :, :], 0.0).then_inc(pads, 1)
            dve.wait_ge(pads, 1)
            dve.memset(m.ve[:, :], 0.0).then_inc(m.started, 1)
            for i in two:
                dve.memset(m.zs[:, :, i, 0:3:2, ER:ER + 1], 1.0).then_inc(pads, 1)
            dve.wait_ge(pads, 3)

            def stack_weights(src, sc, st, layer, chain):
                dve.tensor_scalar(sc[:, :], src[:, :], row_scale[:, layer:layer + 1], None, ALU.mult).then_inc(chain, 1)
                dve.wait_ge(chain, 1)
                dve.tensor_copy(st[:, :], sc[:, :]).then_inc(chain, 1)
                dve.wait_ge(chain, 2)
                lo = slice(2 * SB, SK)
                dve.tensor_tensor(st[lo, :], sc[lo, :], st[lo, :], ALU.subtract).then_inc(m.weights, 1)

            def prepare(g):
                if g == -3:
                    dve.wait_ge(routing_in, 16 * ROUTING_DMAS)
                    split(dve, m.arh[:, :], m.arl[:, :], ar_in[:, :], WS * WS, hi_made[0], m.weights)
                if g == -2:
                    dve.wait_ge(first_in, 16 * FIRST_DMAS)
                    dve.wait_ge(consts, CONSTS)
                    split(dve, m.w1h[:, :], m.w1l[:, :], w1_in[:, :], WS, hi_made[1], m.weights)
                    stack_weights(b1_in, b1_sc, m.b1s, 0, stack_chain[0])
                if g == -1:
                    dve.wait_ge(second_in, 16 * SECOND_DMAS)
                    split(dve, m.w2h[:, :, :], m.w2l[:, :, :], w2_in[:, :, :], WS, hi_made[2], m.weights)
                    stack_weights(b2_in, b2_sc, m.b2s, 1, stack_chain[1])

            def x_ready(e, g):
                for i, (g0, g1) in enumerate(X_PIECES):
                    if not isinstance(g, int) or g0 <= g < g1:
                        e.wait_ge(x_in[i], 16)

            def sequences_ready(e, g):
                e.wait_ge(att.done, 2 * g + 2 if isinstance(g, int) else BATCH)

            run_parts(dve, [
                (ff1.vector(dve, x_ready, prepare), *FF1, {}),
                (att.vector(dve), *ATT, {
                    -3: lambda: dve.wait_ge(ff1.done, 2 * 2),
                    -1: lambda: dve.wait_ge(att_prep, ATT_PREP),
                    0: lambda: dve.wait_ge(ff1.done, 2 * GROUPS),
                    BATCH: lambda: ff2.first_gates()}),
                (ff2.vector(dve, sequences_ready, lambda g: None), *FF2, {})])

        @block.scalar
        def _(act):
            act.wait_ge(consts, 7)
            act.activation(m.ident16[:, :], m.ident32[:, :], ACT.Copy).then_inc(ident16, 1)
            run_parts(act, [
                (ff1.scalar(act), *FF1, {}),
                (att.scalar(act), *ATT_ACT, {
                    -1: lambda: act.wait_ge(att_prep, ATT_PREP),
                    BATCH: lambda: ff2.first_exps()}),
                (ff2.scalar(act), *FF2, {})])

        @block.tensor
        def _(pe):
            pe.wait_ge(consts, 7)
            pe.wait_ge(ident16, 1)

            att_step, begin_attention = att.tensor(pe)

            def begin():
                pe.wait_ge(att_prep, ATT_PREP)
                begin_attention()

            def first_tokens():
                pe.wait_ge(att.yT_lo, BATCH - 1)
                pe.wait_ge(att.squares, 8 * BATCH)

            run_parts(pe, [
                (ff1.tensor(pe), *FF1_PE, {GROUPS: begin}),
                (att_step, *ATT, {0: lambda: pe.wait_ge(ff1.done, 2 * GROUPS)}),
                (ff2.tensor(pe), *FF2, {-2: first_tokens,
                                        -1: lambda: pe.wait_ge(att.yT_lo, BATCH),
                                        0: lambda: pe.wait_ge(att.done, BATCH)})])


_INS = ["L0_attn_x", "L0_attn_Wq", "L0_attn_Wk", "L0_attn_Wv", "L0_attn_Wo", "L0_ffn_W1", "L0_ffn_b1", "L0_ffn_A1",
        "L0_ffn_B1", "L0_ffn_R1", "L0_ffn_W2", "L0_ffn_b2", "L0_ffn_A2", "L0_ffn_B2", "L0_ffn_R2"]


def kernel(**inputs):
    import numpy as np
    from concourse import bacc
    from concourse.bass_utils import run_bass_kernel_spmd

    nc = bacc.Bacc("TRN2", target_bir_lowering=False, num_devices=1)
    arrays, args = {}, []
    for name in _INS:
        a = np.ascontiguousarray(inputs[name])
        arrays[f"in_{name}"] = a
        args.append(nc.dram_tensor(f"in_{name}", a.shape, mybir.dt.from_np(a.dtype), kind="ExternalInput").ap())
    args.append(nc.dram_tensor("out_x", (BATCH, LEN, D), F32, kind="ExternalOutput").ap())
    program(nc, *args)
    return run_bass_kernel_spmd(nc, [arrays], core_ids=[0]).results[0]["out_x"]
```
